# Optimizing a Trainium2 kernel written in Bass

```python
import numpy as np
import jax
import jax.numpy as jnp

def _softmax(x, axis=-1):
    return jax.nn.softmax(x, axis=axis)

def _gelu(x):
    return jax.nn.gelu(x, approximate=True)

def _silu(x):
    return jax.nn.silu(x)

def _sigmoid(x):
    return jax.nn.sigmoid(x)

def _layernorm(x, axis=-1, eps=1e-05):
    m = jnp.mean(x, axis=axis, keepdims=True)
    v = jnp.var(x, axis=axis, keepdims=True)
    return (x - m) / jnp.sqrt(v + eps)

def _scatter_add(tgt, idx, src, axis=0):
    return tgt.at[idx].add(src)

def _segment_sum(src, seg, n):
    return jax.ops.segment_sum(src, seg, n)
kernel_name = 'mk_gnn_ffn_d1_gnn_r32_29fac0'

def setup_inputs(seed: int=0):
    np.random.seed(seed)
    _w = jnp.asarray

    def _rec_inputs():
        import jax
        import jax.numpy as jnp
        _gk = jax.random.key(seed)
        x = -0.0002117 + 1 * jax.random.normal(jax.random.fold_in(_gk, 1), (3125, 256), jnp.float32)
        src = jax.random.randint(jax.random.fold_in(_gk, 2), (50000,), 0, 3125, jnp.int32)
        dst = jax.random.randint(jax.random.fold_in(_gk, 3), (50000,), 0, 3125, jnp.int32)
        _o = jnp.argsort(dst, stable=True)
        src = src[_o]
        dst = dst[_o]
        edge_weight = jax.random.uniform(jax.random.fold_in(_gk, 12), (50000,), jnp.float32, 0.0, 1)
        return (x, src, dst, edge_weight)
    x, src, dst, edge_weight = _rec_inputs()

    def _L0_gnn_setup():
        import jax, jax.numpy as jnp
        import numpy as np
        N_NODES = 3125
        N_EDGES = 100000
        IN_FEATS = 256
        OUT_FEATS = 256
        key = jax.random.key(seed)
        k1, k2, k3, k4, k5, k6 = jax.random.split(key, 6)
        features = jax.random.normal(k1, (N_NODES, IN_FEATS), dtype=jnp.float32)
        edge_src = jax.random.randint(k2, (N_EDGES,), 0, N_NODES, dtype=jnp.int64)
        edge_dst = jnp.sort(jax.random.randint(k3, (N_EDGES,), 0, N_NODES, dtype=jnp.int64))
        edge_weight = jax.random.uniform(k4, (N_EDGES,), dtype=jnp.float32)
        bound = 1.0 / np.sqrt(IN_FEATS)
        W = jax.random.uniform(k5, (OUT_FEATS, IN_FEATS), dtype=jnp.float32, minval=-bound, maxval=bound)
        b = jax.random.uniform(k6, (OUT_FEATS,), dtype=jnp.float32, minval=-bound, maxval=bound)
        return {'features': features, 'edge_src': edge_src, 'edge_dst': edge_dst, 'edge_weight': edge_weight, 'W': W, 'b': b}
    _L0_gnn_all = _L0_gnn_setup()
    _L0_gnn_in = {k: v for k, v in _L0_gnn_all.items() if k in ('W', 'b')}
    del _L0_gnn_all

    def _L0_ffn_setup():
        import jax, jax.numpy as jnp
        import numpy as np
        B, A = (128, 8)
        IN, OUT = (256, 256)
        SH1, SH2 = (256, 128)
        EH1, EH2 = (128, 64)
        E, TOPK = (4, 2)

        def _shared_mlp(x, W1, b1, W2, b2, W3, b3):
            h = jax.nn.relu(x @ W1 + b1)
            h = jax.nn.relu(h @ W2 + b2)
            return h @ W3 + b3

        def _experts_mlp(x, eW1, eb1, eW2, eb2, eW3, eb3):
            h = jax.nn.relu(jnp.einsum('baf,efh->ebah', x, eW1) + eb1[:, None, None, :])
            h = jax.nn.relu(jnp.einsum('ebah,ehg->ebag', h, eW2) + eb2[:, None, None, :])
            o = jnp.einsum('ebag,ego->ebao', h, eW3) + eb3[:, None, None, :]
            return jnp.moveaxis(o, 0, -1)
        key = jax.random.key(seed)
        ks = jax.random.split(key, 16)
        s = 0.05
        return {'x': jax.random.normal(ks[0], (B, A, IN), jnp.float32), 'sW1': jax.random.normal(ks[1], (IN, SH1), jnp.float32) * s, 'sb1': jnp.zeros((SH1,), jnp.float32), 'sW2': jax.random.normal(ks[2], (SH1, SH2), jnp.float32) * s, 'sb2': jnp.zeros((SH2,), jnp.float32), 'sW3': jax.random.normal(ks[3], (SH2, OUT), jnp.float32) * s, 'sb3': jnp.zeros((OUT,), jnp.float32), 'eW1': jax.random.normal(ks[4], (E, IN, EH1), jnp.float32) * s, 'eb1': jnp.zeros((E, EH1), jnp.float32), 'eW2': jax.random.normal(ks[5], (E, EH1, EH2), jnp.float32) * s, 'eb2': jnp.zeros((E, EH2), jnp.float32), 'eW3': jax.random.normal(ks[6], (E, EH2, OUT), jnp.float32) * s, 'eb3': jnp.zeros((E, OUT), jnp.float32), 'gW': jax.random.normal(ks[7], (IN, E), jnp.float32) * s, 'gb': jnp.zeros((E,), jnp.float32)}
    _L0_ffn_all = _L0_ffn_setup()
    _L0_ffn_in = {k: v for k, v in _L0_ffn_all.items() if k in ('sW1', 'sb1', 'sW2', 'sb2', 'sW3', 'sb3', 'eW1', 'eb1', 'eW2', 'eb2', 'eW3', 'eb3', 'gW', 'gb')}
    del _L0_ffn_all
    return {'x': x, 'src': src, 'dst': dst, 'edge_weight': edge_weight, 'L0_gnn_W': _L0_gnn_in['W'], 'L0_gnn_b': _L0_gnn_in['b'], 'L0_ffn_sW1': _L0_ffn_in['sW1'], 'L0_ffn_sb1': _L0_ffn_in['sb1'], 'L0_ffn_sW2': _L0_ffn_in['sW2'], 'L0_ffn_sb2': _L0_ffn_in['sb2'], 'L0_ffn_sW3': _L0_ffn_in['sW3'], 'L0_ffn_sb3': _L0_ffn_in['sb3'], 'L0_ffn_eW1': _L0_ffn_in['eW1'], 'L0_ffn_eb1': _L0_ffn_in['eb1'], 'L0_ffn_eW2': _L0_ffn_in['eW2'], 'L0_ffn_eb2': _L0_ffn_in['eb2'], 'L0_ffn_eW3': _L0_ffn_in['eW3'], 'L0_ffn_eb3': _L0_ffn_in['eb3'], 'L0_ffn_gW': _L0_ffn_in['gW'], 'L0_ffn_gb': _L0_ffn_in['gb']}

def reference(x, src, dst, edge_weight, L0_gnn_W, L0_gnn_b, L0_ffn_sW1, L0_ffn_sb1, L0_ffn_sW2, L0_ffn_sb2, L0_ffn_sW3, L0_ffn_sb3, L0_ffn_eW1, L0_ffn_eb1, L0_ffn_eW2, L0_ffn_eb2, L0_ffn_eW3, L0_ffn_eb3, L0_ffn_gW, L0_ffn_gb):
    import jax
    import jax.numpy as jnp

    def _L0_gnn_ref(features, edge_src, edge_dst, edge_weight, W, b):
        import jax, jax.numpy as jnp
        import numpy as np
        N_NODES = 3125
        N_EDGES = 100000
        IN_FEATS = 256
        OUT_FEATS = 256
        msgs = features[edge_src] * edge_weight[:, None]
        agg = jax.ops.segment_sum(msgs, edge_dst, num_segments=N_NODES, indices_are_sorted=True)
        return jnp.einsum('ni,oi->no', agg, W) + b

    def _L0_ffn_ref(x, sW1, sb1, sW2, sb2, sW3, sb3, eW1, eb1, eW2, eb2, eW3, eb3, gW, gb):
        import jax, jax.numpy as jnp
        import numpy as np
        B, A = (128, 8)
        IN, OUT = (256, 256)
        SH1, SH2 = (256, 128)
        EH1, EH2 = (128, 64)
        E, TOPK = (4, 2)

        def _shared_mlp(x, W1, b1, W2, b2, W3, b3):
            h = jax.nn.relu(x @ W1 + b1)
            h = jax.nn.relu(h @ W2 + b2)
            return h @ W3 + b3

        def _experts_mlp(x, eW1, eb1, eW2, eb2, eW3, eb3):
            h = jax.nn.relu(jnp.einsum('baf,efh->ebah', x, eW1) + eb1[:, None, None, :])
            h = jax.nn.relu(jnp.einsum('ebah,ehg->ebag', h, eW2) + eb2[:, None, None, :])
            o = jnp.einsum('ebag,ego->ebao', h, eW3) + eb3[:, None, None, :]
            return jnp.moveaxis(o, 0, -1)
        all_out = _experts_mlp(x, eW1, eb1, eW2, eb2, eW3, eb3)
        shared = _shared_mlp(x, sW1, sb1, sW2, sb2, sW3, sb3)
        gates = jax.nn.softmax(x @ gW + gb, axis=-1)
        topv, topi = jax.lax.top_k(gates, TOPK)
        topw = jax.nn.softmax(topv, axis=-1)
        sel = jnp.take_along_axis(all_out, topi[:, :, None, :], axis=-1)
        gated = jnp.sum(sel * topw[:, :, None, :], axis=-1)
        return shared + gated
    x = x + _L0_gnn_ref(_layernorm(x, axis=-1), src, dst, edge_weight, L0_gnn_W, L0_gnn_b)
    x = x + _L0_ffn_ref(_layernorm(x, axis=-1)[None], L0_ffn_sW1, L0_ffn_sb1, L0_ffn_sW2, L0_ffn_sb2, L0_ffn_sW3, L0_ffn_sb3, L0_ffn_eW1, L0_ffn_eb1, L0_ffn_eW2, L0_ffn_eb2, L0_ffn_eW3, L0_ffn_eb3, L0_ffn_gW, L0_ffn_gb)[0]
    return x

_drawn_inputs = setup_inputs


def setup_inputs(seed=0):
    import zlib

    import numpy as np

    out = dict(_drawn_inputs(seed))
    spreads = {'L0_ffn_sb1': (0.0, 0.671),
     'L0_ffn_sb2': (0.0, 0.318),
     'L0_ffn_sb3': (0.0, 0.1),
     'L0_ffn_eb1': (0.0, 0.8),
     'L0_ffn_eb2': (0.0, 0.794),
     'L0_ffn_eb3': (0.0, 0.1),
     'L0_ffn_gb': (0.0, 0.615)}
    factors = {}
    for name, (base, spread) in spreads.items():
        noise = np.random.default_rng([zlib.crc32(name.encode()), seed]).standard_normal(out[name].shape)
        drawn = base * np.exp(spread * noise) if base else spread * noise
        out[name] = jnp.asarray(drawn.astype(out[name].dtype))
    for name, factor in factors.items():
        out[name] = (out[name] * factor).astype(out[name].dtype)
    return out
```

```python
from contextlib import ExitStack

import concourse.bass as bass
from concourse import mybir

P = 128
F32 = mybir.dt.float32
BF16 = mybir.dt.bfloat16
I32 = mybir.dt.int32
ALU = mybir.AluOpType
ACT = mybir.ActivationFunctionType
AX_X = mybir.AxisListType.X
LN_EPS = 1e-5

N_NODES, N_EDGES, D = 3125, 50000, 256
KD = D // P
N_TILES = -(-N_NODES // P)
TAIL = N_NODES - (N_TILES - 1) * P
PAIR = 2 * P
N_PAIRS = N_NODES // PAIR
N_CHUNKS = -(-N_EDGES // P)
TAIL_EDGES = N_EDGES - (N_CHUNKS - 1) * P
STEP = 8
BATCH = 8
PER_PAIR = PAIR // STEP
BATCHES = PER_PAIR // BATCH
COLS = -(-N_CHUNKS // BATCH) * BATCH
MARGIN = 32
WINDOW = STEP + 2 * MARGIN
LAST_CHUNKS = N_CHUNKS - N_PAIRS * PER_PAIR
E = 4
H1 = 6
GEN = 4
assert N_EDGES == N_NODES * P // STEP and LAST_CHUNKS <= BATCH and COLS % GEN == 0


def build(nc, x, src, src_tail, dst, dst_tail, wgt, wgt_tail, gnn_wt, gnn_b, sw1, ew1, b1,
          sw2, ew2, b2, sw3, ew3, b3, gate_w, gate_b, out, force_general=False):
    table = nc.dram_tensor("normalised_rows", [N_NODES, D], F32)

    with ExitStack() as ctx:
        def sb(name, shape, dt=F32):
            return ctx.enter_context(nc.sbuf_tensor(name, shape, dt))

        def bank(name):
            return ctx.enter_context(nc.psum_tensor(name, [P, 512], F32))

        def sem(name):
            return ctx.enter_context(nc.semaphore(name))

        x_sb = sb("x_sb", [P, N_TILES, D])
        xn_all = sb("xn_all", [P, N_TILES, D])
        stats0 = sb("stats0", [P, N_TILES, 6])
        mv0 = sb("mv0", [P, N_TILES, 2])
        std0 = sb("std0", [P, N_TILES])
        rstd0 = sb("rstd0", [P, N_TILES])
        shift0 = sb("shift0", [P, N_TILES])
        eps = sb("eps", [P, 1])
        src_all = sb("src_all", [P, COLS], I32)
        dst_i = sb("dst_i", [P, COLS], I32)
        dst_f = sb("dst_f", [P, COLS])
        rel_all = sb("rel_all", [P, COLS])
        w_all = sb("w_all", [P, COLS])
        starts = sb("starts", [P, COLS])
        away = sb("away", [P, COLS])
        away_max = sb("away_max", [P, 1])
        farthest = sb("farthest", [1, 1])
        flag = sb("flag", [1, 1], I32)
        src_now = sb("src_now", [P, 2, PER_PAIR], I32)
        rel_now = sb("rel_now", [P, 2, PER_PAIR])
        w_now = sb("w_now", [P, 2, PER_PAIR])
        rows = sb("rows", [P, PER_PAIR, D])
        select = sb("select", [P, PER_PAIR, WINDOW])
        ident = sb("ident", [P, P])
        iota = sb("iota", [P, P])
        before = sb("before", [P, E, E])
        owner = sb("owner", [E + 1, 2, P])
        zero_l = sb("zero_l", [1, P], BF16)
        zero_r = sb("zero_r", [1, 512], BF16)
        gnn_wt_sb = sb("gnn_wt_sb", [P, KD, D])
        gnn_b_sb = sb("gnn_b_sb", [P, D])
        sw1_sb = sb("sw1_sb", [P, KD, D])
        ew1_sb = sb("ew1_sb", [P, KD, E, P])
        b1_sb = sb("b1_sb", [P, H1])
        sw2_sb = sb("sw2_sb", [P, KD, P])
        ew2_sb = sb("ew2_sb", [P, E, P])
        b2_sb = sb("b2_sb", [P, 3])
        sw3_sb = sb("sw3_sb", [P, D])
        ew3_sb = sb("ew3_sb", [P, 2, D])
        b3_sb = sb("b3_sb", [E + 1, D])
        gate_w_sb = sb("gate_w_sb", [P, KD, E])
        gate_b_sb = sb("gate_b_sb", [P, E])
        agg_sb = sb("agg_sb", [P, KD, PAIR])
        x1 = sb("x1", [P, 2, D])
        stats = sb("stats", [P, 2, 6])
        mv = sb("mv", [P, 2, 2])
        std = sb("std", [P, 2])
        rstd = sb("rstd", [P, 2])
        xn = sb("xn", [P, 2, D])
        xt = sb("xt", [P, KD, PAIR])
        logit = sb("logit", [P, 2, E])
        top = sb("top", [P, 2])
        low = sb("low", [P, 2, E])
        ex = sb("ex", [P, 2, E])
        total = sb("total", [P, 2])
        inv = sb("inv", [P, 2])
        gate = sb("gate", [P, 2, E])
        gtop = sb("gtop", [P, 2])
        glow = sb("glow", [P, 2, E])
        gex = sb("gex", [P, 2, E])
        ahead = sb("ahead", [P, 2, E, E])
        tied = sb("tied", [P, 2, E, E])
        rank = sb("rank", [P, 2, E])
        kept = sb("kept", [P, 2, E])
        ktotal = sb("ktotal", [P, 2])
        kinv = sb("kinv", [P, 2])
        mix = sb("mix", [P, 2, E + 1])
        mix_t = sb("mix_t", [E + 1, PAIR])
        h1 = sb("h1", [P, H1, PAIR])
        h2 = sb("h2", [P, 3, PAIR])
        y = sb("y", [P, 2, D])
        agg_all = sb("agg_all", [P, KD, N_TILES * P])

        agg_ps = [bank("agg_even"), bank("agg_odd")]
        tok_ps = bank("tok_ps")
        mid_ps = bank("mid_ps")
        hid_ps = [bank(f"hid{k}_ps") for k in range(3)]
        gate_ps = bank("gate_ps")
        shared2_ps, experts2_ps = hid_ps[0], hid_ps[1]

        gen_select = select[:, :, :].rearrange("p j n -> p (j n)")[:, 0:GEN * P].rearrange(
            "p (j n) -> p j n", j=GEN)

        def by_half(t):
            return t[:, :].rearrange("p (k n) -> p k n", k=2)

        LG = 0
        MT = P

        s_x = [sem(f"s_x{g}") for g in range(7)]
        s_edges = sem("s_edges")
        s_w = sem("s_w")
        s_pad = sem("s_pad")
        s_const = sem("s_const")
        s_pre = sem("s_pre")
        s_edge = sem("s_edge")
        s_resid = sem("s_resid")
        s_std0 = sem("s_std0")
        s_normed_v = sem("s_normed_v")
        s_normed_a = sem("s_normed_a")
        s_table = sem("s_table")
        s_away = sem("s_away")
        s_away_t = sem("s_away_t")
        s_flag = sem("s_flag")
        s_staged = sem("s_staged")
        s_rows = [sem(f"s_rows{j}") for j in range(PER_PAIR)]
        s_select = [sem(f"s_select{b}") for b in range(BATCHES)]
        s_used = [sem(f"s_used{b}") for b in range(BATCHES)]
        s_summed = sem("s_summed")
        s_agg = sem("s_agg")
        steps_of_pair = (
            "lin x1 stats var std rstd xn turned xt logits h1a h1b l2 h2 mix mix_turned spread mixt mixed end y "
            "logit top low ex total inv gate gtop ahead tied tied_before glow gex order rank kept "
            "ktotal kinv").split()
        s = {n: sem("ffn_" + n) for n in steps_of_pair}
        s_l1 = [sem(f"s_l1_{k}") for k in range(3)]
        s_held = {n: sem(f"s_held_{n}") for n in ("pool", "pe", "dve")}
        s_out = sem("s_out")
        s_gen_rows = [sem(f"s_gen_rows{j}") for j in range(GEN)]
        s_gen_idx = sem("s_gen_idx")
        s_gen_rel = sem("s_gen_rel")
        s_gen_sel = sem("s_gen_sel")
        s_gen_sum = sem("s_gen_sum")
        s_gen_add = sem("s_gen_add")

        groups = [(4 * g, 4) for g in range(6)] + [(N_TILES - 1, 1)]
        N_LOADS = 16

        block = ctx.enter_context(nc.Block())

        def tile_shape(tiles):
            return (2, P, PAIR) if tiles == 2 else (1, TAIL, TAIL)

        @block.sync
        def _(sp):
            for g, (t0, n) in enumerate(groups):
                if n == 4:
                    sp.dma_start(x_sb[:, t0:t0 + n, :],
                                 x[t0 * P:(t0 + n) * P, :].rearrange("(t p) d -> p t d", p=P)
                                 ).then_inc(s_x[g], 16)
                else:
                    sp.dma_start(x_sb[0:TAIL, t0, :], x[t0 * P:N_NODES, :]).then_inc(s_x[g], 16)
            for g, (t0, n) in enumerate(groups):
                sp.wait_ge(s_normed_v, g + 1)
                sp.wait_ge(s_normed_a, min(g + 1, 6))
                if n == 4:
                    sp.dma_start(table[t0 * P:(t0 + n) * P, :].rearrange("(t p) d -> p t d", p=P),
                                 xn_all[:, t0:t0 + n, :]).then_inc(s_table, 16)
                else:
                    sp.dma_start(table[t0 * P:N_NODES, :], xn_all[0:TAIL, t0, :]).then_inc(s_table, 16)

            def store(q, tiles):
                sp.wait_ge(s["y"], q + 1)
                if tiles == 2:
                    sp.dma_start(out[bass.ds(q * PAIR, PAIR), :].rearrange("(t p) d -> p t d", p=P),
                                 y[:, :, :]).then_inc(s_out, 16)
                else:
                    sp.dma_start(out[N_PAIRS * PAIR:N_NODES, :], y[0:TAIL, 0, :]).then_inc(s_out, 16)

            with sp.Fori(0, N_PAIRS) as q:
                store(q, 2)
            store(N_PAIRS, 1)
            sp.wait_ge(s_out, 16 * (N_PAIRS + 1))

        @block.gpsimd
        def _(pool):
            pool.iota(starts[:, :], pattern=[[STEP, COLS]], base=-MARGIN, channel_multiplier=0,
                      allow_small_or_imprecise_dtypes=True).then_inc(s_const, 1)
            pool.iota(iota[:, :], pattern=[[1, P]], base=0, channel_multiplier=0,
                      allow_small_or_imprecise_dtypes=True).then_inc(s_const, 1)
            pool.memset(ident[:, :], 0.0).then_inc(s_const, 1)
            pool.memset(before[:, :, :], 1.0).then_inc(s_const, 1)
            pool.memset(owner[:, :, :], 1.0).then_inc(s_const, 1)
            pool.wait_ge(s_const, 5)
            pool.affine_select(out=ident[:, :], in_=ident[:, :], compare_op=ALU.not_equal, fill=1.0,
                               base=0, pattern=[[-1, P]], channel_multiplier=1).then_inc(s_const, 1)
            pool.affine_select(out=before[:, :, :], in_=before[:, :, :], compare_op=ALU.is_gt,
                               fill=0.0, base=0, pattern=[[1, E], [-1, E]],
                               channel_multiplier=0).then_inc(s_const, 1)
            pool.affine_select(out=owner[:, :, :], in_=owner[:, :, :], compare_op=ALU.is_ge,
                               fill=0.0, base=0, pattern=[[P, 2], [1, P]],
                               channel_multiplier=-64).then_inc(s_const, 1)
            pool.wait_ge(s_const, 8)
            pool.affine_select(out=owner[:, :, :], in_=owner[:, :, :], compare_op=ALU.is_ge,
                               fill=0.0, base=63, pattern=[[-P, 2], [-1, P]],
                               channel_multiplier=64).then_inc(s_const, 1)
            pool.wait_ge(s_table, 16 * len(groups))
            pool.wait_ge(s_flag, 1)

            def gather_pair(i, parity, chunks=PER_PAIR):
                pool.wait_ge(s_staged, i + 1)
                pool.sem_inc(s_held["pool"], 1)
                for j in range(chunks):
                    if j % BATCH == 0 and not (isinstance(i, int) and i == 0):
                        pool.wait_ge(s_used[j // BATCH], i)
                        pool.sem_inc(s_held["pool"], 1)
                    pool.indirect_dma_start(
                        rows[:, j, :], None, table[:, :],
                        bass.IndirectOffsetOnAxis(ap=src_now[:, parity, j:j + 1], axis=0)
                    ).then_inc(s_rows[j], 16)

            with pool.If(pool.value_load(flag[0:1, 0:1], min_val=0, max_val=1)):
                with pool.Fori(0, COLS // GEN) as g:
                    pool.wait_ge(s_gen_idx, g + 1)
                    pool.sem_inc(s_held["pool"], 1)
                    for j in range(GEN):
                        pool.indirect_dma_start(
                            rows[:, j, :], None, table[:, :],
                            bass.IndirectOffsetOnAxis(ap=src_now[:, 0, j:j + 1], axis=0)
                        ).then_inc(s_gen_rows[j], 16)
            with pool.Else():
                gather_pair(0, 0)
                gather_pair(1, 1)
                with pool.Fori(2, N_PAIRS, 2) as i:
                    gather_pair(i, 0)
                    gather_pair(i + 1, 1)
                gather_pair(N_PAIRS, 0, LAST_CHUNKS)

        @block.scalar
        def _(act):
            def load(dst_ap, src_ap, signal=s_w):
                act.dma_start(dst_ap, src_ap).then_inc(signal, 16)

            act.wait_ge(s_pad, 3)
            for whole, tail, to in ((dst, dst_tail, dst_i), (src, src_tail, src_all),
                                    (wgt, wgt_tail, w_all)):
                load(to[:, 0:N_CHUNKS - 1], whole, s_edges)
                load(to[0:TAIL_EDGES, N_CHUNKS - 1:N_CHUNKS], tail, s_edges)
            act.wait_ge(s_pad, 6)
            load(gnn_b_sb[:, :], gnn_b.to_broadcast([P, D]))
            load(gnn_wt_sb[:, :, :], gnn_wt.rearrange("(k p) n -> p k n", p=P))
            load(gate_w_sb[:, :, :], gate_w.rearrange("(k p) n -> p k n", p=P))
            load(gate_b_sb[:, :], gate_b.to_broadcast([P, E]))
            load(sw1_sb[:, :, :], sw1.rearrange("(k p) n -> p k n", p=P))
            load(ew1_sb[:, :, :, :], ew1)
            for e in range(E):
                half = 64 * (e % 2)
                load(ew2_sb[:, e, half:half + 64], ew2[e])
            load(b1_sb[:, :], b1)
            load(sw2_sb[:, :, :], sw2.rearrange("(k p) n -> p k n", p=P))
            load(b2_sb[:, :], b2)
            load(sw3_sb[:, :], sw3)
            load(ew3_sb[:, :, :], ew3)
            load(b3_sb[:, :], b3)

            for g, (t0, n) in enumerate(groups):
                r = P if n == 4 else TAIL
                act.wait_ge(s_pre, 4 * g + 2)
                act.activation(std0[0:r, t0:t0 + n], mv0[0:r, t0:t0 + n, 1], ACT.Sqrt,
                               bias=eps[0:r, :]).then_inc(s_std0, 1)
                if n == 4:
                    act.wait_ge(s_pre, 4 * g + 4)
                    for t in (t0 + 1, t0 + 3):
                        last = act.activation(xn_all[:, t, :], x_sb[:, t, :], ACT.Identity,
                                              bias=shift0[:, t:t + 1], scale=rstd0[:, t:t + 1])
                    last.then_inc(s_normed_a, 1)

            def copy_sums(q, parity, tok=PAIR):
                act.wait_ge(s_summed, q + 1)
                if not (isinstance(q, int) and q == 0):
                    act.wait_ge(s["lin"], q)
                act.activation(agg_sb[:, :, 0:tok], by_half(agg_ps[parity])[:, :, 0:tok],
                               ACT.Copy).then_inc(s_agg, 1)

            def ffn(q, tiles):
                T, r, tok = tile_shape(tiles)
                first = isinstance(q, int) and q == 0
                n = q + 1
                act.wait_ge(s["var"], n)
                act.activation(std[0:r, 0:T], mv[0:r, 0:T, 1], ACT.Sqrt,
                               bias=eps[0:r, :]).then_inc(s["std"], 1)
                act.wait_ge(s["turned"], n)
                if not first:
                    act.wait_ge(s_l1[2], q)
                act.activation(xt[:, :, 0:tok], by_half(mid_ps)[:, :, 0:tok],
                               ACT.Copy).then_inc(s["xt"], 1)
                act.wait_ge(s["low"], n)
                act.activation(ex[0:r, 0:T, :], low[0:r, 0:T, :], ACT.Exp).then_inc(s["ex"], 1)
                if not first:
                    act.wait_ge(s["l2"], q)
                for k in range(2):
                    act.wait_ge(s_l1[k], n)
                    for m in (2 * k, 2 * k + 1):
                        last = act.activation(h1[:, m, 0:tok], by_half(hid_ps[k])[:, m % 2, 0:tok],
                                              ACT.Relu, bias=b1_sb[:, m:m + 1])
                last.then_inc(s["h1a"], 1)
                act.wait_ge(s["glow"], n)
                act.activation(gex[0:r, 0:T, :], glow[0:r, 0:T, :], ACT.Exp).then_inc(s["gex"], 1)
                act.wait_ge(s["l2"], n)
                if not first:
                    act.wait_ge(s["end"], q)
                act.activation(h2[:, 0, 0:tok], shared2_ps[:, 0:tok], ACT.Relu, bias=b2_sb[:, 0:1])
                for k in range(2):
                    last = act.activation(h2[:, 1 + k, 0:tok], by_half(experts2_ps)[:, k, 0:tok],
                                          ACT.Relu, bias=b2_sb[:, 1 + k:2 + k])
                last.then_inc(s["h2"], 1)

            act.wait_ge(s_flag, 1)
            with act.If(act.value_load(flag[0:1, 0:1], min_val=0, max_val=1)):
                ffn(0, 2)
                with act.Fori(1, N_PAIRS) as q:
                    ffn(q, 2)
                ffn(N_PAIRS, 1)
            with act.Else():
                copy_sums(0, 0)
                ffn(0, 2)
                with act.Fori(1, N_PAIRS - 1, 2) as q:
                    copy_sums(q, 1)
                    ffn(q, 2)
                    copy_sums(q + 1, 0)
                    ffn(q + 1, 2)
                copy_sums(N_PAIRS - 1, 1)
                ffn(N_PAIRS - 1, 2)
                copy_sums(N_PAIRS, 0, TAIL)
                ffn(N_PAIRS, 1)

        @block.tensor
        def _(pe):
            pe.wait_ge(s_const, 9)
            pe.wait_ge(s_away, 1)
            pe.transpose(mid_ps[0:1, 0:P], away_max[:, :], ident[:, :]).then_inc(s_away_t, 1)
            pe.wait_ge(s_flag, 1)
            pe.wait_ge(s_w, 16 * N_LOADS)
            pe.wait_ge(s_pad, 8)

            def clear(parity):
                return pe.matmul(agg_ps[parity][:, :], zero_l[:, :], zero_r[:, :], start=True,
                                 stop=False, skip_group_check=True)

            def add_chunk(j, parity, low_part, high_part):
                a = STEP * j - MARGIN
                parts = [(parity, max(a, 0), min(a + WINDOW, PAIR), max(-a, 0))]
                if a < 0 and low_part:
                    parts.append((1 - parity, PAIR + a, PAIR, 0))
                if a + WINDOW > PAIR and high_part:
                    parts.append((1 - parity, 0, a + WINDOW - PAIR, PAIR - a))
                for bk, c0, c1, s0 in parts:
                    for k in range(KD):
                        last = pe.matmul(agg_ps[bk][:, k * PAIR + c0:k * PAIR + c1],
                                         rows[:, j, k * P:(k + 1) * P],
                                         select[:, j, s0:s0 + c1 - c0],
                                         start=False, stop=False, skip_group_check=True)
                return last

            def ffn(q, tiles):
                T, r, tok = tile_shape(tiles)
                first = isinstance(q, int) and q == 0
                n = q + 1

                def linear():
                    pe.wait_ge(s_agg, n)
                    if not first:
                        pe.wait_ge(s["y"], q)
                    for t in range(T):
                        for k in range(KD):
                            last = pe.matmul(tok_ps[0:r, t * D:(t + 1) * D],
                                             agg_sb[:, k, t * P:t * P + r], gnn_wt_sb[:, k, :],
                                             start=(k == 0), stop=(k == KD - 1))
                    last.then_inc(s["lin"], 1)

                def turn():
                    pe.wait_ge(s["xn"], n)
                    if not first:
                        pe.wait_ge(s["mixt"], q)
                    for t in range(T):
                        for k in range(KD):
                            last = pe.transpose(mid_ps[:, k * PAIR + t * P:k * PAIR + t * P + r],
                                                xn[0:r, t, k * P:(k + 1) * P], ident[0:r, 0:r])
                    last.then_inc(s["turned"], 1)

                def logits():
                    pe.wait_ge(s["xt"], n)
                    for t in range(T):
                        for k in range(KD):
                            last = pe.matmul(mid_ps[0:r, LG + t * E:LG + (t + 1) * E],
                                             xt[:, k, t * P:t * P + r], gate_w_sb[:, k, :],
                                             start=(k == 0), stop=(k == KD - 1))
                    last.then_inc(s["logits"], 1)

                def layer1(b):
                    if not first:
                        pe.wait_ge(s["h2"] if b < 2 else s["h1b"], q)
                    for m in (2 * b, 2 * b + 1):
                        for k in range(KD):
                            w = sw1_sb[:, k, m * P:(m + 1) * P] if m < 2 else ew1_sb[:, k, m - 2, :]
                            last = pe.matmul(by_half(hid_ps[b])[:, m % 2, 0:tok], w, xt[:, k, 0:tok],
                                             start=(k == 0), stop=(k == KD - 1))
                    last.then_inc(s_l1[b], 1)

                def layer2():
                    pe.wait_ge(s["h1a"], n)
                    pe.wait_ge(s["h1b"], n)
                    for k in range(KD):
                        pe.matmul(shared2_ps[:, 0:tok], sw2_sb[:, k, :], h1[:, k, 0:tok],
                                  start=(k == 0), stop=(k == KD - 1))
                    for e in range(E):
                        last = pe.matmul(by_half(experts2_ps)[:, e // 2, 0:tok], ew2_sb[:, e, :],
                                         h1[:, 2 + e, 0:tok], start=(e % 2 == 0), stop=(e % 2 == 1))
                    last.then_inc(s["l2"], 1)

                def turn_gates():
                    pe.wait_ge(s["mix"], n)
                    for t in range(T):
                        last = pe.transpose(mid_ps[0:E + 1, MT + t * P:MT + t * P + r],
                                            mix[0:r, t, :], ident[0:r, 0:r])
                    last.then_inc(s["mix_turned"], 1)

                def spread():
                    pe.wait_ge(s["mixt"], n)
                    for k in range(2):
                        last = pe.matmul(by_half(gate_ps)[:, k, 0:tok], owner[:, k, :],
                                         mix_t[:, 0:tok], start=True, stop=True)
                    last.then_inc(s["spread"], 1)

                def layer3():
                    pe.wait_ge(s["mixed"], n)
                    pe.wait_ge(s["x1"], n)
                    for t in range(T):
                        o = tok_ps[0:r, t * D:(t + 1) * D]
                        c = slice(t * P, t * P + r)
                        pe.matmul(o, h2[:, 0, c], sw3_sb[:, :], start=True, stop=False)
                        for k in range(2):
                            pe.matmul(o, h2[:, 1 + k, c], ew3_sb[:, k, :], start=False, stop=False)
                        last = pe.matmul(o, mix_t[:, c], b3_sb[:, :], start=False, stop=True)
                    last.then_inc(s["end"], 1)

                return {5: [linear], 10: [turn], 13: [logits, lambda: layer1(0)],
                        14: [lambda: layer1(1)], 15: [lambda: layer1(2)], 18: [layer2],
                        20: [turn_gates], 22: [spread], 26: [layer3]}

            def run(steps):
                for at in sorted(steps):
                    for step in steps[at]:
                        step()

            def pair(i, parity, chunks=PER_PAIR):
                first = isinstance(i, int) and i == 0
                steps = {} if first else ffn(i - 1, 2)
                for j in range(chunks):
                    if j % BATCH == 0:
                        pe.wait_ge(s_select[j // BATCH], i + 1)
                    pe.wait_ge(s_rows[j], 16 * (i + 1))
                    last = add_chunk(j, parity, not first, chunks == PER_PAIR)
                    if STEP * j == MARGIN - STEP and not first:
                        last.then_inc(s_summed, 1)
                    elif j % BATCH == BATCH - 1:
                        last.then_inc(s_used[j // BATCH], 1)
                    if j == chunks - 1 and chunks < PER_PAIR:
                        last.then_inc(s_summed, 1)
                    if j == 26:
                        if not first:
                            pe.wait_ge(s_agg, i)
                        clear(1 - parity)
                    for step in steps.pop(j, []):
                        step()
                run(steps)

            with pe.If(pe.value_load(flag[0:1, 0:1], min_val=0, max_val=1)):
                with pe.Fori(0, COLS // GEN) as g:
                    for j in range(GEN):
                        pe.wait_ge(s_gen_rows[j], 16 * (g + 1))
                    pe.sem_inc(s_held["pe"], 1)
                    with pe.Fori(0, N_TILES) as t:
                        step = g * N_TILES + t + 1
                        pe.wait_ge(s_gen_sel, step)
                        for k in range(KD):
                            for j in range(GEN):
                                last = pe.matmul(agg_ps[0][:, k * P:(k + 1) * P],
                                                 rows[:, j, k * P:(k + 1) * P],
                                                 gen_select[:, j, :],
                                                 start=(j == 0), stop=(j == GEN - 1))
                        last.then_inc(s_gen_sum, 1)
                run(ffn(0, 2))
                with pe.Fori(1, N_PAIRS) as q:
                    run(ffn(q, 2))
                run(ffn(N_PAIRS, 1))
            with pe.Else():
                clear(0)
                pair(0, 0)
                pair(1, 1)
                with pe.Fori(2, N_PAIRS, 2) as i:
                    pair(i, 0)
                    pair(i + 1, 1)
                pair(N_PAIRS, 0, LAST_CHUNKS)
                run(ffn(N_PAIRS, 1))

        @block.vector
        def _(dve):
            dve.memset(dst_i[:, N_CHUNKS - 1:COLS], N_NODES - 1).then_inc(s_pad, 1)
            dve.memset(src_all[:, N_CHUNKS - 1:COLS], 0).then_inc(s_pad, 1)
            dve.memset(w_all[:, N_CHUNKS - 1:COLS], 0.0).then_inc(s_pad, 1)
            dve.memset(ew2_sb[:, :, :], 0.0).then_inc(s_pad, 1)
            dve.memset(zero_l[:, :], 0.0).then_inc(s_pad, 1)
            dve.memset(zero_r[:, :], 0.0).then_inc(s_pad, 1)
            dve.memset(mix[:, :, :], 1.0).then_inc(s_pad, 1)
            dve.memset(eps[:, :], LN_EPS).then_inc(s_pad, 1)

            def stage(i, parity, n=PER_PAIR):
                if not (isinstance(i, int) and i < 2):
                    dve.wait_ge(s_used[BATCHES - 1], i - 1)
                c = bass.ds(i * PER_PAIR, n)
                dve.tensor_copy(src_now[:, parity, 0:n], src_all[:, c])
                dve.tensor_copy(rel_now[:, parity, 0:n], rel_all[:, c])
                dve.tensor_copy(w_now[:, parity, 0:n], w_all[:, c]).then_inc(s_staged, 1)

            def selectors(i, b, parity):
                if b == 0:
                    dve.wait_ge(s_staged, i + 1)
                if not (isinstance(i, int) and i == 0):
                    dve.wait_ge(s_used[b], i)
                for j in range(b * BATCH, (b + 1) * BATCH):
                    last = dve.tensor_scalar(select[:, j, :], iota[:, 0:WINDOW],
                                             rel_now[:, parity, j:j + 1], w_now[:, parity, j:j + 1],
                                             ALU.is_equal, ALU.mult)
                last.then_inc(s_select[b], 1)

            for g, (t0, n) in enumerate(groups):
                r = P if n == 4 else TAIL
                if g == 0:
                    dve.wait_ge(s_pad, 8)
                dve.wait_ge(s_x[g], 16)
                for t in range(t0, t0 + n):
                    last = dve.bn_stats(stats0[0:r, t, :], x_sb[0:r, t, :])
                last.then_inc(s_pre, 1)
                dve.wait_ge(s_pre, 4 * g + 1)
                for t in range(t0, t0 + n):
                    last = dve.bn_aggr(mv0[0:r, t, :], stats0[0:r, t, :])
                last.then_inc(s_pre, 1)
                dve.wait_ge(s_std0, g + 1)
                dve.reciprocal(rstd0[0:r, t0:t0 + n], std0[0:r, t0:t0 + n]).then_inc(s_pre, 1)
                dve.wait_ge(s_pre, 4 * g + 3)
                dve.scalar_tensor_tensor(out=shift0[0:r, t0:t0 + n], in0=mv0[0:r, t0:t0 + n, 0],
                                         scalar=-1.0, in1=rstd0[0:r, t0:t0 + n],
                                         op0=ALU.mult, op1=ALU.mult).then_inc(s_pre, 1)
                dve.wait_ge(s_pre, 4 * g + 4)
                for t in range(t0, t0 + n, 2):
                    last = dve.tensor_scalar(xn_all[0:r, t, :], x_sb[0:r, t, :], mv0[0:r, t, 0:1],
                                             rstd0[0:r, t:t + 1], ALU.subtract, ALU.mult)
                last.then_inc(s_normed_v, 1)
            dve.wait_ge(s_edges, 16 * 6)
            dve.wait_ge(s_const, 9)
            dve.tensor_copy(dst_f[:, :], dst_i[:, :]).then_inc(s_edge, 1)
            dve.wait_ge(s_edge, 1)
            dve.tensor_tensor(rel_all[:, :], dst_f[:, :], starts[:, :], ALU.subtract).then_inc(s_edge, 1)
            dve.wait_ge(s_edge, 2)
            dve.tensor_scalar(away[:, :], rel_all[:, :], (WINDOW - 1) / 2, None,
                              ALU.subtract).then_inc(s_edge, 1)
            dve.wait_ge(s_edge, 3)
            dve.tensor_reduce(away_max[:, :], away[:, :], AX_X, ALU.max,
                              apply_absolute_value=True).then_inc(s_away, 1)
            dve.wait_ge(s_away_t, 1)
            dve.tensor_reduce(farthest[:, :], mid_ps[0:1, 0:P], AX_X, ALU.max).then_inc(s_away, 1)
            dve.wait_ge(s_away, 2)
            dve.tensor_scalar(flag[:, :], farthest[:, :], -1.0 if force_general else WINDOW / 2, None,
                              ALU.is_gt).then_inc(s_flag, 1)
            dve.wait_ge(s_w, 16 * N_LOADS)
            dve.wait_ge(s_normed_a, 6)
            dve.tensor_tensor(x_sb[:, 0:N_TILES - 1, :], x_sb[:, 0:N_TILES - 1, :],
                              gnn_b_sb[:, :].unsqueeze(1).to_broadcast([P, N_TILES - 1, D]), ALU.add)
            dve.tensor_tensor(x_sb[0:TAIL, N_TILES - 1, :], x_sb[0:TAIL, N_TILES - 1, :],
                              gnn_b_sb[0:TAIL, :], ALU.add).then_inc(s_resid, 1)
            dve.wait_ge(s_resid, 1)
            dve.wait_ge(s_flag, 1)

            def ffn(q, tiles):
                T, r, tok = tile_shape(tiles)
                first = isinstance(q, int) and q == 0
                n = q + 1
                flat = "p t d -> p (t d)"

                def residual():
                    dve.wait_ge(s["lin"], n)
                    if not first:
                        dve.wait_ge(s["y"], q)
                    dve.tensor_tensor(x1[0:r, 0:T, :], by_half(tok_ps)[0:r, 0:T, :],
                                      x_sb[0:r, bass.ds(q * 2, T), :], ALU.add).then_inc(s["x1"], 1)
                    dve.wait_ge(s["x1"], n)
                    for t in range(T):
                        last = dve.bn_stats(stats[0:r, t, :], x1[0:r, t, :])
                    last.then_inc(s["stats"], 1)
                    dve.wait_ge(s["stats"], n)
                    dve.sem_inc(s_held["dve"], 1)
                    for t in range(T):
                        last = dve.bn_aggr(mv[0:r, t, :], stats[0:r, t, :])
                    last.then_inc(s["var"], 1)
                    dve.wait_ge(s["std"], n)
                    dve.reciprocal(rstd[0:r, 0:T], std[0:r, 0:T]).then_inc(s["rstd"], 1)
                    dve.wait_ge(s["rstd"], n)
                    if not first:
                        dve.wait_ge(s["turned"], q)
                    for t in range(T):
                        last = dve.tensor_scalar(xn[0:r, t, :], x1[0:r, t, :], mv[0:r, t, 0:1],
                                                 rstd[0:r, t:t + 1], ALU.subtract, ALU.mult)
                    last.then_inc(s["xn"], 1)

                def route():
                    R = slice(0, r), slice(0, T)
                    each = [r, T, E]
                    two = [r, T, E, E]

                    def wide(v):
                        return v[R].unsqueeze(2).to_broadcast(each)

                    dve.wait_ge(s["logits"], n)
                    dve.tensor_tensor(logit[R], mid_ps[0:r, LG:LG + T * E].rearrange(
                        "p (t e) -> p t e", e=E), gate_b_sb[0:r, :].unsqueeze(1).to_broadcast(each),
                        ALU.add).then_inc(s["logit"], 1)
                    dve.wait_ge(s["logit"], n)
                    dve.tensor_reduce(top[R], logit[R], AX_X, ALU.max).then_inc(s["top"], 1)
                    dve.wait_ge(s["top"], n)
                    dve.tensor_tensor(low[R], logit[R], wide(top), ALU.subtract).then_inc(s["low"], 1)
                    dve.wait_ge(s["ex"], n)
                    dve.tensor_reduce(total[R], ex[R], AX_X, ALU.add).then_inc(s["total"], 1)
                    dve.wait_ge(s["total"], n)
                    dve.reciprocal(inv[R], total[R]).then_inc(s["inv"], 1)
                    dve.wait_ge(s["inv"], n)
                    dve.tensor_tensor(gate[R], ex[R], wide(inv), ALU.mult).then_inc(s["gate"], 1)
                    dve.wait_ge(s["gate"], n)
                    dve.tensor_reduce(gtop[R], gate[R], AX_X, ALU.max).then_inc(s["gtop"], 1)
                    a = gate[R].unsqueeze(3).to_broadcast(two)
                    b = gate[R].unsqueeze(2).to_broadcast(two)
                    dve.tensor_tensor(ahead[R], b, a, ALU.is_gt).then_inc(s["ahead"], 1)
                    dve.tensor_tensor(tied[R], b, a, ALU.is_equal).then_inc(s["tied"], 1)
                    dve.wait_ge(s["tied"], n)
                    dve.tensor_tensor(glow[R], gate[R], wide(gtop), ALU.subtract).then_inc(s["glow"], 1)
                    dve.tensor_tensor(tied[R], tied[R],
                                      before[0:r, :, :].unsqueeze(1).to_broadcast(two),
                                      ALU.mult).then_inc(s["tied_before"], 1)
                    dve.wait_ge(s["tied_before"], n)
                    dve.tensor_tensor(ahead[R], ahead[R], tied[R], ALU.add).then_inc(s["order"], 1)
                    dve.wait_ge(s["order"], n)
                    dve.tensor_reduce(rank[R], ahead[R], AX_X, ALU.add).then_inc(s["rank"], 1)
                    dve.wait_ge(s["rank"], n)
                    dve.wait_ge(s["gex"], n)
                    dve.scalar_tensor_tensor(out=kept[R], in0=rank[R], scalar=1.5, in1=gex[R],
                                             op0=ALU.is_lt, op1=ALU.mult).then_inc(s["kept"], 1)
                    dve.wait_ge(s["kept"], n)
                    dve.tensor_reduce(ktotal[R], kept[R], AX_X, ALU.add).then_inc(s["ktotal"], 1)
                    dve.wait_ge(s["ktotal"], n)
                    dve.reciprocal(kinv[R], ktotal[R]).then_inc(s["kinv"], 1)
                    dve.wait_ge(s["kinv"], n)
                    if not first:
                        dve.wait_ge(s["mix_turned"], q)
                    dve.tensor_tensor(mix[0:r, 0:T, 0:E], kept[R], wide(kinv),
                                      ALU.mult).then_inc(s["mix"], 1)

                def relu1():
                    if not first:
                        dve.wait_ge(s["l2"], q)
                    dve.wait_ge(s_l1[2], n)
                    for m in (4, 5):
                        last = dve.tensor_scalar(h1[:, m, 0:tok], by_half(hid_ps[2])[:, m % 2, 0:tok],
                                                 b1_sb[:, m:m + 1], 0.0, ALU.add, ALU.max)
                    last.then_inc(s["h1b"], 1)

                def weigh():
                    dve.wait_ge(s["mix_turned"], n)
                    if not first:
                        dve.wait_ge(s["end"], q)
                    dve.tensor_copy(mix_t[:, 0:tok], mid_ps[0:E + 1, MT:MT + tok]).then_inc(s["mixt"], 1)
                    dve.wait_ge(s["h2"], n)
                    dve.wait_ge(s["spread"], n)
                    dve.tensor_tensor(h2[:, 1:3, 0:tok], h2[:, 1:3, 0:tok],
                                      by_half(gate_ps)[:, :, 0:tok], ALU.mult).then_inc(s["mixed"], 1)

                def finish():
                    dve.wait_ge(s["end"], n)
                    if not first:
                        dve.wait_ge(s_out, 16 * q)
                    dve.tensor_tensor(y[0:r, 0:T, :], by_half(tok_ps)[0:r, 0:T, :], x1[0:r, 0:T, :],
                                      ALU.add).then_inc(s["y"], 1)

                return residual, (lambda: (route(), relu1())), weigh, finish

            def pair(i, parity, next_n=PER_PAIR):
                first = isinstance(i, int) and i == 0
                steps = () if first else ffn(i - 1, 2)
                stage(i + 1, 1 - parity, next_n)
                for b in range(BATCHES):
                    if b < BATCHES - 1:
                        selectors(i, b + 1, parity)
                    else:
                        selectors(i + 1, 0, 1 - parity)
                    if not first:
                        steps[b]()

            def fetch_sums(q, n=PAIR):
                if not (isinstance(q, int) and q == 0):
                    dve.wait_ge(s["lin"], q)
                dve.tensor_copy(agg_sb[:, :, 0:n],
                                agg_all[:, :, bass.ds(q * PAIR, n)]).then_inc(s_agg, 1)

            with dve.If(dve.value_load(flag[0:1, 0:1], min_val=0, max_val=1)):
                dve.memset(agg_all[:, :, :], 0.0).then_inc(s_gen_add, 1)
                with dve.Fori(0, COLS // GEN) as g:
                    dve.wait_ge(s_gen_add, g * N_TILES + 1)
                    c = bass.ds(g * GEN, GEN)
                    dve.tensor_copy(w_now[:, 0, 0:GEN], w_all[:, c])
                    dve.tensor_copy(rel_now[:, 0, 0:GEN], dst_f[:, c]).then_inc(s_gen_rel, 1)
                    dve.tensor_copy(src_now[:, 0, 0:GEN], src_all[:, c]).then_inc(s_gen_idx, 1)
                    with dve.Fori(0, N_TILES) as t:
                        step = g * N_TILES + t + 1
                        dve.wait_ge(s_gen_rel, g * (N_TILES + 1) + t + 1)
                        dve.wait_ge(s_gen_add, step)
                        for j in range(GEN):
                            last = dve.tensor_scalar(gen_select[:, j, :], iota[:, :],
                                                     rel_now[:, 0, j:j + 1], w_now[:, 0, j:j + 1],
                                                     ALU.is_equal, ALU.mult)
                        last.then_inc(s_gen_sel, 1)
                        dve.wait_ge(s_gen_sel, step)
                        dve.tensor_scalar(rel_now[:, 0, 0:GEN], rel_now[:, 0, 0:GEN], float(P), None,
                                          ALU.subtract).then_inc(s_gen_rel, 1)
                        dve.wait_ge(s_gen_sum, step)
                        so_far = agg_all[:, :, bass.ds(t * P, P)]
                        dve.tensor_tensor(so_far, so_far,
                                          agg_ps[0][:, 0:KD * P].rearrange("p (k n) -> p k n", k=KD),
                                          ALU.add).then_inc(s_gen_add, 1)
                dve.wait_ge(s_gen_add, (COLS // GEN) * N_TILES + 1)
                fetch_sums(0)
                for step in ffn(0, 2):
                    step()
                with dve.Fori(1, N_PAIRS) as q:
                    fetch_sums(q)
                    for step in ffn(q, 2):
                        step()
                fetch_sums(N_PAIRS, TAIL)
                for step in ffn(N_PAIRS, 1):
                    step()
            with dve.Else():
                stage(0, 0)
                selectors(0, 0, 0)
                pair(0, 0)
                pair(1, 1)
                with dve.Fori(2, N_PAIRS - 2, 2) as i:
                    pair(i, 0)
                    pair(i + 1, 1)
                pair(N_PAIRS - 2, 0)
                pair(N_PAIRS - 1, 1, BATCH)
                for step in ffn(N_PAIRS - 1, 2):
                    step()
                for step in ffn(N_PAIRS, 1):
                    step()


def kernel(x, src, dst, edge_weight, L0_gnn_W, L0_gnn_b, L0_ffn_sW1, L0_ffn_sb1, L0_ffn_sW2,
           L0_ffn_sb2, L0_ffn_sW3, L0_ffn_sb3, L0_ffn_eW1, L0_ffn_eb1, L0_ffn_eW2, L0_ffn_eb2,
           L0_ffn_eW3, L0_ffn_eb3, L0_ffn_gW, L0_ffn_gb):
    import numpy as np
    import concourse.bacc as bacc
    from concourse.bass_utils import run_bass_kernel_spmd

    def chunks(a):
        a = np.asarray(a)
        whole = (N_CHUNKS - 1) * P
        return a[:whole].reshape(N_CHUNKS - 1, P).T, a[whole:].reshape(TAIL_EDGES, 1)

    def row(a):
        return np.asarray(a).reshape(1, -1)

    ew1 = np.asarray(L0_ffn_eW1).reshape(E, KD, P, P).transpose(2, 1, 0, 3)
    ew3 = np.asarray(L0_ffn_eW3).reshape(2, P, D).transpose(1, 0, 2)
    b1 = np.concatenate([np.asarray(L0_ffn_sb1).reshape(2, P), np.asarray(L0_ffn_eb1)]).T
    b2 = np.concatenate([row(L0_ffn_sb2), np.asarray(L0_ffn_eb2).reshape(2, P)]).T
    b3 = np.concatenate([np.asarray(L0_ffn_eb3), row(L0_ffn_sb3)])
    laid = [x, *chunks(src), *chunks(dst), *chunks(edge_weight), np.asarray(L0_gnn_W).T, row(L0_gnn_b),
            L0_ffn_sW1, ew1, b1, L0_ffn_sW2, L0_ffn_eW2, b2, L0_ffn_sW3, ew3, b3, L0_ffn_gW,
            row(L0_ffn_gb)]
    names = ["x", "src", "src_tail", "dst", "dst_tail", "wgt", "wgt_tail", "gnn_wt", "gnn_b", "sw1",
             "ew1", "b1", "sw2", "ew2", "b2", "sw3", "ew3", "b3", "gate_w", "gate_b"]
    nc = bacc.Bacc("TRN2", target_bir_lowering=False, num_devices=1)
    arrays, args = {}, []
    for name, a in zip(names, laid):
        a = np.ascontiguousarray(a)
        arrays[f"in_{name}"] = a
        args.append(nc.dram_tensor(f"in_{name}", a.shape, mybir.dt.from_np(a.dtype),
                                   kind="ExternalInput").ap())
    out = nc.dram_tensor("out", (N_NODES, D), F32, kind="ExternalOutput").ap()
    build(nc, *args, out)
    return run_bass_kernel_spmd(nc, [arrays], core_ids=[0]).results[0]["out"]
```

```python
from contextlib import ExitStack

import concourse.bass as bass
from concourse import mybir

P = 128
F32 = mybir.dt.float32
BF16 = mybir.dt.bfloat16
I32 = mybir.dt.int32
ALU = mybir.AluOpType
ACT = mybir.ActivationFunctionType
AX_X = mybir.AxisListType.X
LN_EPS = 1e-5

N_NODES, N_EDGES, D = 3125, 50000, 256
KD = D // P
N_TILES = -(-N_NODES // P)
TAIL = N_NODES - (N_TILES - 1) * P
PAIR = 2 * P
N_PAIRS = N_NODES // PAIR
N_CHUNKS = -(-N_EDGES // P)
TAIL_EDGES = N_EDGES - (N_CHUNKS - 1) * P
STEP = 8
BATCH = 8
PER_PAIR = PAIR // STEP
BATCHES = PER_PAIR // BATCH
COLS = -(-N_CHUNKS // BATCH) * BATCH
MARGIN = 44
WINDOW = STEP + 2 * MARGIN
LAST_CHUNKS = N_CHUNKS - N_PAIRS * PER_PAIR
LOW = -(-MARGIN // STEP)
CARRY = STEP * (max(LOW, LAST_CHUNKS) - 1) + STEP + MARGIN
SUMS = PAIR + CARRY
E = 4
H1 = 6
GEN = 4
assert N_EDGES == N_NODES * P // STEP and COLS % GEN == 0 and SUMS <= 512
assert LOW < LAST_CHUNKS <= BATCH and CARRY >= TAIL


def build(nc, x, ends, ends_tail, wgt, wgt_tail, gnn_wt, gnn_b, sw1, ew1, b1,
          sw2, ew2, b2, sw3, ew3, b3, gate_w, gate_b, out, force_general=False):
    table = nc.dram_tensor("normalised_rows", [N_NODES, D], F32)

    with ExitStack() as ctx:
        def sb(name, shape, dt=F32):
            return ctx.enter_context(nc.sbuf_tensor(name, shape, dt))

        def bank(name):
            return ctx.enter_context(nc.psum_tensor(name, [P, 512], F32))

        def sem(name):
            return ctx.enter_context(nc.semaphore(name))

        x_sb = sb("x_sb", [P, N_TILES, D])
        xn_all = sb("xn_all", [P, N_TILES, D])
        stats0 = sb("stats0", [P, N_TILES, 6])
        mv0 = sb("mv0", [P, N_TILES, 2])
        std0 = sb("std0", [P, N_TILES])
        rstd0 = sb("rstd0", [P, N_TILES])
        row_stats = sb("row_stats", [P, PER_PAIR, 6])
        row_mv = sb("row_mv", [P, PER_PAIR, 2])
        row_std = sb("row_std", [P, PER_PAIR])
        row_rstd = sb("row_rstd", [P, PER_PAIR])
        row_shift = sb("row_shift", [P, PER_PAIR])
        shift0 = sb("shift0", [P, N_TILES])
        eps = sb("eps", [P, 1])
        ends_all = sb("ends_all", [P, COLS, 2], I32)
        src_all, dst_i = ends_all[:, :, 0], ends_all[:, :, 1]
        dst_f = sb("dst_f", [P, COLS])
        rel_all = sb("rel_all", [P, COLS])
        w_all = sb("w_all", [P, COLS])
        starts = sb("starts", [P, COLS])
        away = sb("away", [P, COLS])
        away_max = sb("away_max", [P, 1])
        farthest = sb("farthest", [1, 1])
        flag = sb("flag", [1, 1], I32)
        src_now = sb("src_now", [P, 2, PER_PAIR], I32)
        rel_now = sb("rel_now", [P, 2, PER_PAIR])
        w_now = sb("w_now", [P, 2, PER_PAIR])
        rows = sb("rows", [P, PER_PAIR, D])
        select = sb("select", [P, PER_PAIR, WINDOW])
        ident = sb("ident", [P, P])
        iota = sb("iota", [P, P])
        before = sb("before", [P, E, E])
        owner = sb("owner", [E + 1, 2, P])
        zero_l = sb("zero_l", [1, P], BF16)
        zero_r = sb("zero_r", [1, 512], BF16)
        gnn_wt_sb = sb("gnn_wt_sb", [P, KD, D])
        gnn_b_sb = sb("gnn_b_sb", [P, D])
        sw1_sb = sb("sw1_sb", [P, KD, D])
        ew1_sb = sb("ew1_sb", [P, KD, E, P])
        b1_sb = sb("b1_sb", [P, H1])
        sw2_sb = sb("sw2_sb", [P, KD, P])
        ew2_sb = sb("ew2_sb", [P, E, P])
        b2_sb = sb("b2_sb", [P, 3])
        sw3_sb = sb("sw3_sb", [P, D])
        ew3_sb = sb("ew3_sb", [P, 2, D])
        b3_sb = sb("b3_sb", [E + 1, D])
        gate_w_sb = sb("gate_w_sb", [P, KD, E])
        gate_b_sb = sb("gate_b_sb", [P, E])
        sums = [sb(f"sums{k}", [P, KD, SUMS]) for k in range(2)]
        x1 = sb("x1", [P, 2, D])
        stats = sb("stats", [P, 2, 6])
        mv = sb("mv", [P, 2, 2])
        std = sb("std", [P, 2])
        rstd = sb("rstd", [P, 2])
        xn = sb("xn", [P, 2, D])
        xt = sb("xt", [P, KD, PAIR])
        logit = sb("logit", [P, 2, E])
        top = sb("top", [P, 2])
        low = sb("low", [P, 2, E])
        ex = sb("ex", [P, 2, E])
        total = sb("total", [P, 2])
        inv = sb("inv", [P, 2])
        gate = sb("gate", [P, 2, E])
        gtop = sb("gtop", [P, 2])
        glow = sb("glow", [P, 2, E])
        gex = sb("gex", [P, 2, E])
        ahead = sb("ahead", [P, 2, E, E])
        tied = sb("tied", [P, 2, E, E])
        rank = sb("rank", [P, 2, E])
        kept = sb("kept", [P, 2, E])
        ktotal = sb("ktotal", [P, 2])
        kinv = sb("kinv", [P, 2])
        mix = sb("mix", [P, 2, E + 1])
        mix_t = sb("mix_t", [E + 1, PAIR])
        h1 = sb("h1", [P, H1, PAIR])
        h2 = sb("h2", [P, 3, PAIR])
        y = sb("y", [P, 2, D])
        agg_all = sb("agg_all", [P, KD, N_TILES * P])

        agg_ps = [ctx.enter_context(nc.psum_tensor(f"agg{k}_ps", [P, KD, 512], F32)) for k in range(2)]
        tok_ps = bank("tok_ps")
        mid_ps = bank("mid_ps")
        hid_ps = [bank(f"hid{k}_ps") for k in range(2)]
        experts2_ps, shared2_ps = hid_ps

        gen_select = select[:, :, :].rearrange("p j n -> p (j n)")[:, 0:GEN * P].rearrange(
            "p (j n) -> p j n", j=GEN)

        def by_half(t):
            return t[:, :].rearrange("p (k n) -> p k n", k=2)

        LG = 0
        MT = P

        s_x = [sem(f"s_x{g}") for g in range(7)]
        s_ends = sem("s_ends")
        s_edges = sem("s_edges")
        s_w = sem("s_w")
        s_pad = sem("s_pad")
        s_const = sem("s_const")
        s_stats0 = sem("s_stats0")
        s_var0 = sem("s_var0")
        s_std0 = sem("s_std0")
        s_rstd0 = sem("s_rstd0")
        s_shift0 = sem("s_shift0")
        s_normed = sem("s_normed")
        s_normed_v = sem("s_normed_v")
        s_row_stats = sem("s_row_stats")
        s_row_var = sem("s_row_var")
        s_row_std = sem("s_row_std")
        s_row_rstd = sem("s_row_rstd")
        s_row_shift = sem("s_row_shift")
        s_row_normed = sem("s_row_normed")
        s_edge = sem("s_edge")
        s_resid = sem("s_resid")
        s_table = sem("s_table")
        s_away = sem("s_away")
        s_away_t = sem("s_away_t")
        s_flag = sem("s_flag")
        s_src = sem("s_src")
        s_staged = sem("s_staged")
        s_rows = [sem(f"s_rows{j}") for j in range(PER_PAIR)]
        s_select = [sem(f"s_select{b}") for b in range(BATCHES)]
        s_used = [sem(f"s_used{b}") for b in range(BATCHES)]
        s_summed = sem("s_summed")
        s_copied = sem("s_copied")
        s_combined = sem("s_combined")
        steps_of_pair = (
            "lin x1 stats var std rstd xn turned xt logits h1a h1b h1 l2 h2 mix mix_turned spread mixt mixed end y "
            "logit top low ex total inv gate gtop ahead tied tied_before glow gex order rank kept "
            "ktotal kinv").split()
        s = {n: sem("ffn_" + n) for n in steps_of_pair}
        s_l1 = [sem(f"s_l1_{k}") for k in range(3)]
        s_held = {n: sem(f"s_held_{n}") for n in ("pool", "pe", "dve")}
        s_out = sem("s_out")
        s_gen_rows = [sem(f"s_gen_rows{j}") for j in range(GEN)]
        s_gen_idx = sem("s_gen_idx")
        s_gen_rel = sem("s_gen_rel")
        s_gen_sel = sem("s_gen_sel")
        s_gen_sum = sem("s_gen_sum")
        s_gen_add = sem("s_gen_add")

        groups = [(4 * g, 4) for g in range(6)] + [(N_TILES - 1, 1)]
        N_LOADS = 16

        block = ctx.enter_context(nc.Block())

        def tile_shape(tiles):
            return (2, P, PAIR) if tiles == 2 else (1, TAIL, TAIL)

        @block.sync
        def _(sp):
            sp.dma_start(ends_all[:, 0:N_CHUNKS - 1, :], ends).then_inc(s_ends, 16)
            sp.dma_start(w_all[:, 0:N_CHUNKS - 1], wgt).then_inc(s_edges, 16)
            for g, (t0, n) in enumerate(groups):
                if n == 4:
                    sp.dma_start(x_sb[:, t0:t0 + n, :],
                                 x[t0 * P:(t0 + n) * P, :].rearrange("(t p) d -> p t d", p=P)
                                 ).then_inc(s_x[g], 16)
                else:
                    sp.dma_start(x_sb[0:TAIL, t0, :], x[t0 * P:N_NODES, :]).then_inc(s_x[g], 16)
            for g, (t0, n) in enumerate(groups):
                sp.wait_ge(s_normed, g + 1)
                sp.wait_ge(s_normed_v, min(g + 1, 6))
                if n == 4:
                    sp.dma_start(table[t0 * P:(t0 + n) * P, :].rearrange("(t p) d -> p t d", p=P),
                                 xn_all[:, t0:t0 + n, :]).then_inc(s_table, 16)
                else:
                    sp.dma_start(table[t0 * P:N_NODES, :], xn_all[0:TAIL, t0, :]).then_inc(s_table, 16)

            def load(dst_ap, src_ap):
                sp.dma_start(dst_ap, src_ap).then_inc(s_w, 16)

            sp.wait_ge(s_pad, 6)
            load(gnn_b_sb[:, :], gnn_b.to_broadcast([P, D]))
            load(gnn_wt_sb[:, :, :], gnn_wt.rearrange("(k p) n -> p k n", p=P))
            load(gate_w_sb[:, :, :], gate_w.rearrange("(k p) n -> p k n", p=P))
            load(gate_b_sb[:, :], gate_b.to_broadcast([P, E]))
            load(sw1_sb[:, :, :], sw1.rearrange("(k p) n -> p k n", p=P))
            load(ew1_sb[:, :, :, :], ew1)
            for e in range(E):
                half = 64 * (e % 2)
                load(ew2_sb[:, e, half:half + 64], ew2[e])
            load(b1_sb[:, :], b1)
            load(sw2_sb[:, :, :], sw2.rearrange("(k p) n -> p k n", p=P))
            load(b2_sb[:, :], b2)
            load(sw3_sb[:, :], sw3)
            load(ew3_sb[:, :, :], ew3)
            load(b3_sb[:, :], b3)

            def store(q, tiles):
                sp.wait_ge(s["y"], q + 1)
                if tiles == 2:
                    sp.dma_start(out[bass.ds(q * PAIR, PAIR), :].rearrange("(t p) d -> p t d", p=P),
                                 y[:, :, :]).then_inc(s_out, 16)
                else:
                    sp.dma_start(out[N_PAIRS * PAIR:N_NODES, :], y[0:TAIL, 0, :]).then_inc(s_out, 16)

            with sp.Fori(0, N_PAIRS) as q:
                store(q, 2)
            store(N_PAIRS, 1)
            sp.wait_ge(s_out, 16 * (N_PAIRS + 1))

        @block.gpsimd
        def _(pool):
            pool.iota(starts[:, :], pattern=[[STEP, COLS]], base=-MARGIN, channel_multiplier=0,
                      allow_small_or_imprecise_dtypes=True).then_inc(s_const, 1)
            pool.iota(iota[:, :], pattern=[[1, P]], base=0, channel_multiplier=0,
                      allow_small_or_imprecise_dtypes=True).then_inc(s_const, 1)
            pool.memset(ident[:, :], 0.0).then_inc(s_const, 1)
            pool.memset(before[:, :, :], 1.0).then_inc(s_const, 1)
            pool.memset(owner[:, :, :], 1.0).then_inc(s_const, 1)
            pool.wait_ge(s_const, 5)
            pool.affine_select(out=ident[:, :], in_=ident[:, :], compare_op=ALU.not_equal, fill=1.0,
                               base=0, pattern=[[-1, P]], channel_multiplier=1).then_inc(s_const, 1)
            pool.affine_select(out=before[:, :, :], in_=before[:, :, :], compare_op=ALU.is_gt,
                               fill=0.0, base=0, pattern=[[1, E], [-1, E]],
                               channel_multiplier=0).then_inc(s_const, 1)
            pool.affine_select(out=owner[:, :, :], in_=owner[:, :, :], compare_op=ALU.is_ge,
                               fill=0.0, base=0, pattern=[[P, 2], [1, P]],
                               channel_multiplier=-64).then_inc(s_const, 1)
            pool.wait_ge(s_const, 8)
            pool.affine_select(out=owner[:, :, :], in_=owner[:, :, :], compare_op=ALU.is_ge,
                               fill=0.0, base=63, pattern=[[-P, 2], [-1, P]],
                               channel_multiplier=64).then_inc(s_const, 1)
            pool.wait_ge(s_src, 1)
            for j in range(PER_PAIR):
                pool.indirect_dma_start(
                    rows[:, j, :], None, x[:, :],
                    bass.IndirectOffsetOnAxis(ap=src_now[:, 0, j:j + 1], axis=0)
                ).then_inc(s_rows[j], 16)
            pool.wait_ge(s_table, 16 * len(groups))
            pool.wait_ge(s_flag, 1)

            def gather_pair(i, parity, chunks=PER_PAIR):
                pool.wait_ge(s_staged, i + 1)
                pool.sem_inc(s_held["pool"], 1)
                for j in range(chunks):
                    if j % BATCH == 0:
                        pool.wait_ge(s_used[j // BATCH], i)
                        pool.sem_inc(s_held["pool"], 1)
                    pool.indirect_dma_start(
                        rows[:, j, :], None, table[:, :],
                        bass.IndirectOffsetOnAxis(ap=src_now[:, parity, j:j + 1], axis=0)
                    ).then_inc(s_rows[j], 16)

            with pool.If(pool.value_load(flag[0:1, 0:1], min_val=0, max_val=1)):
                for j in range(GEN):
                    pool.wait_ge(s_rows[j], 16)
                with pool.Fori(0, COLS // GEN) as g:
                    pool.wait_ge(s_gen_idx, g + 1)
                    pool.sem_inc(s_held["pool"], 1)
                    for j in range(GEN):
                        pool.indirect_dma_start(
                            rows[:, j, :], None, table[:, :],
                            bass.IndirectOffsetOnAxis(ap=src_now[:, 1, j:j + 1], axis=0)
                        ).then_inc(s_gen_rows[j], 16)
            with pool.Else():
                gather_pair(1, 1)
                with pool.Fori(2, N_PAIRS, 2) as i:
                    gather_pair(i, 0)
                    gather_pair(i + 1, 1)
                gather_pair(N_PAIRS, 0, LAST_CHUNKS)

        @block.scalar
        def _(act):
            act.wait_ge(s_pad, 2)
            act.dma_start(ends_all[0:TAIL_EDGES, N_CHUNKS - 1:N_CHUNKS, :],
                          ends_tail).then_inc(s_edges, 16)
            act.dma_start(w_all[0:TAIL_EDGES, N_CHUNKS - 1:N_CHUNKS], wgt_tail).then_inc(s_edges, 16)

            act.wait_ge(s_pad, 7)
            for g, (t0, n) in enumerate(groups):
                r = P if n == 4 else TAIL
                act.wait_ge(s_var0, g + 1)
                act.activation(std0[0:r, t0:t0 + n], mv0[0:r, t0:t0 + n, 1], ACT.Sqrt,
                               bias=eps[0:r, :]).then_inc(s_std0, 1)
                act.wait_ge(s_shift0, g + 1)
                for t in range(t0, t0 + min(n, 3)):
                    last = act.activation(xn_all[0:r, t, :], x_sb[0:r, t, :], ACT.Identity,
                                          bias=shift0[0:r, t:t + 1], scale=rstd0[0:r, t:t + 1])
                last.then_inc(s_normed, 1)

            def normalise_rows(b):
                c = slice(b * BATCH, (b + 1) * BATCH)
                act.wait_ge(s_row_var, b + 1)
                act.activation(row_std[:, c], row_mv[:, c, 1], ACT.Sqrt,
                               bias=eps[:, :]).then_inc(s_row_std, 1)
                act.wait_ge(s_row_shift, b + 1)
                for j in range(b * BATCH, (b + 1) * BATCH):
                    last = act.activation(rows[:, j, :], rows[:, j, :], ACT.Identity,
                                          bias=row_shift[:, j:j + 1], scale=row_rstd[:, j:j + 1])
                last.then_inc(s_row_normed, 1)

            def copy_sums(q, parity):
                act.wait_ge(s_summed, q + 1)
                if not (isinstance(q, int) and q == 0):
                    act.wait_ge(s["lin"], q)
                act.activation(sums[parity][:, :, :], agg_ps[parity][:, :, 0:SUMS],
                               ACT.Copy).then_inc(s_copied, 1)

            def ffn(q, tiles):
                T, r, tok = tile_shape(tiles)
                first = isinstance(q, int) and q == 0
                n = q + 1
                act.wait_ge(s["var"], n)
                act.activation(std[0:r, 0:T], mv[0:r, 0:T, 1], ACT.Sqrt,
                               bias=eps[0:r, :]).then_inc(s["std"], 1)
                act.wait_ge(s["turned"], n)
                if not first:
                    act.wait_ge(s_l1[2], q)
                act.activation(xt[:, :, 0:tok], by_half(mid_ps)[:, :, 0:tok],
                               ACT.Copy).then_inc(s["xt"], 1)
                act.wait_ge(s["low"], n)
                act.activation(ex[0:r, 0:T, :], low[0:r, 0:T, :], ACT.Exp).then_inc(s["ex"], 1)
                if not first:
                    act.wait_ge(s["l2"], q)

                def relu1(k):
                    act.wait_ge(s_l1[k], n)
                    for m in (2 * k, 2 * k + 1):
                        last = act.activation(h1[:, m, 0:tok], by_half(hid_ps[k % 2])[:, m % 2, 0:tok],
                                              ACT.Relu, bias=b1_sb[:, m:m + 1])
                    last.then_inc(s[("h1a", "h1b", "h1")[k]], 1)

                relu1(0)
                act.wait_ge(s["glow"], n)
                act.activation(gex[0:r, 0:T, :], glow[0:r, 0:T, :], ACT.Exp).then_inc(s["gex"], 1)
                relu1(1)
                relu1(2)
                act.wait_ge(s["l2"], n)
                if not first:
                    act.wait_ge(s["end"], q)
                act.activation(h2[:, 0, 0:tok], shared2_ps[:, 0:tok], ACT.Relu, bias=b2_sb[:, 0:1])
                for k in range(2):
                    last = act.activation(h2[:, 1 + k, 0:tok], by_half(experts2_ps)[:, k, 0:tok],
                                          ACT.Relu, bias=b2_sb[:, 1 + k:2 + k])
                last.then_inc(s["h2"], 1)

            act.wait_ge(s_flag, 1)
            with act.If(act.value_load(flag[0:1, 0:1], min_val=0, max_val=1)):
                ffn(0, 2)
                with act.Fori(1, N_PAIRS) as q:
                    ffn(q, 2)
                ffn(N_PAIRS, 1)
            with act.Else():
                for b in range(BATCHES):
                    normalise_rows(b)
                copy_sums(0, 0)
                ffn(0, 2)
                with act.Fori(1, N_PAIRS - 1, 2) as q:
                    copy_sums(q, 1)
                    ffn(q, 2)
                    copy_sums(q + 1, 0)
                    ffn(q + 1, 2)
                copy_sums(N_PAIRS - 1, 1)
                ffn(N_PAIRS - 1, 2)
                ffn(N_PAIRS, 1)

        @block.tensor
        def _(pe):
            pe.wait_ge(s_const, 9)
            pe.wait_ge(s_away, 1)
            pe.transpose(mid_ps[0:1, 0:P], away_max[:, :], ident[:, :]).then_inc(s_away_t, 1)
            pe.wait_ge(s_flag, 1)
            pe.wait_ge(s_w, 16 * N_LOADS)
            pe.wait_ge(s_pad, 7)

            def clear(parity):
                for k in range(KD):
                    pe.matmul(agg_ps[parity][:, k, 0:SUMS], zero_l[:, :], zero_r[:, 0:SUMS],
                              start=True, stop=False, skip_group_check=True)

            def add_chunk(j, parity, first_node):
                skip = max(-first_node, 0)
                for k in range(KD):
                    last = pe.matmul(agg_ps[parity][:, k, first_node + skip:first_node + WINDOW],
                                     rows[:, j, k * P:(k + 1) * P], select[:, j, skip:],
                                     start=False, stop=False, skip_group_check=True)
                return last

            def ffn(q, tiles, ready, sums_q):
                T, r, tok = tile_shape(tiles)
                first = isinstance(q, int) and q == 0
                n = q + 1

                def linear():
                    pe.wait_ge(ready[0], ready[1])
                    if not first:
                        pe.wait_ge(s["y"], q)
                    for t in range(T):
                        for k in range(KD):
                            last = pe.matmul(tok_ps[0:r, t * D:(t + 1) * D],
                                             sums_q[:, k, t * P:t * P + r],
                                             gnn_wt_sb[:, k, :], start=(k == 0), stop=(k == KD - 1))
                    last.then_inc(s["lin"], 1)

                def turn():
                    pe.wait_ge(s["xn"], n)
                    if not first:
                        pe.wait_ge(s["mixt"], q)
                    for t in range(T):
                        for k in range(KD):
                            last = pe.transpose(mid_ps[:, k * PAIR + t * P:k * PAIR + t * P + r],
                                                xn[0:r, t, k * P:(k + 1) * P], ident[0:r, 0:r])
                    last.then_inc(s["turned"], 1)

                def logits():
                    pe.wait_ge(s["xt"], n)
                    for t in range(T):
                        for k in range(KD):
                            last = pe.matmul(mid_ps[0:r, LG + t * E:LG + (t + 1) * E],
                                             xt[:, k, t * P:t * P + r], gate_w_sb[:, k, :],
                                             start=(k == 0), stop=(k == KD - 1))
                    last.then_inc(s["logits"], 1)

                def layer1(b):
                    if b == 2:
                        pe.wait_ge(s["h1a"], n)
                    elif not first:
                        pe.wait_ge(s["h2"], q)
                    for m in (2 * b, 2 * b + 1):
                        for k in range(KD):
                            w = sw1_sb[:, k, m * P:(m + 1) * P] if m < 2 else ew1_sb[:, k, m - 2, :]
                            last = pe.matmul(by_half(hid_ps[b % 2])[:, m % 2, 0:tok], w, xt[:, k, 0:tok],
                                             start=(k == 0), stop=(k == KD - 1))
                    last.then_inc(s_l1[b], 1)

                def layer2():
                    pe.wait_ge(s["h1"], n)
                    for k in range(KD):
                        pe.matmul(shared2_ps[:, 0:tok], sw2_sb[:, k, :], h1[:, k, 0:tok],
                                  start=(k == 0), stop=(k == KD - 1))
                    for e in range(E):
                        last = pe.matmul(by_half(experts2_ps)[:, e // 2, 0:tok], ew2_sb[:, e, :],
                                         h1[:, 2 + e, 0:tok], start=(e % 2 == 0), stop=(e % 2 == 1))
                    last.then_inc(s["l2"], 1)

                def turn_gates():
                    pe.wait_ge(s["mix"], n)
                    for t in range(T):
                        last = pe.transpose(mid_ps[0:E + 1, MT + t * P:MT + t * P + r],
                                            mix[0:r, t, :], ident[0:r, 0:r])
                    last.then_inc(s["mix_turned"], 1)

                def spread():
                    pe.wait_ge(s["mixt"], n)
                    pe.wait_ge(s["x1"], n)
                    for k in range(2):
                        last = pe.matmul(by_half(tok_ps)[:, k, 0:tok], owner[:, k, :],
                                         mix_t[:, 0:tok], start=True, stop=True)
                    last.then_inc(s["spread"], 1)

                def layer3():
                    pe.wait_ge(s["mixed"], n)
                    for t in range(T):
                        o = tok_ps[0:r, t * D:(t + 1) * D]
                        c = slice(t * P, t * P + r)
                        pe.matmul(o, h2[:, 0, c], sw3_sb[:, :], start=True, stop=False)
                        for k in range(2):
                            pe.matmul(o, h2[:, 1 + k, c], ew3_sb[:, k, :], start=False, stop=False)
                        last = pe.matmul(o, mix_t[:, c], b3_sb[:, :], start=False, stop=True)
                    last.then_inc(s["end"], 1)

                return {LOW + 4: [linear], 15: [turn], 18: [logits, lambda: layer1(0)],
                        19: [lambda: layer1(1)], 20: [lambda: layer1(2)], 23: [layer2],
                        26: [turn_gates], 28: [spread], 31: [layer3]}

            def run(steps):
                for at in sorted(steps):
                    for step in steps[at]:
                        step()

            def pair(i, parity, chunks=PER_PAIR):
                first = isinstance(i, int) and i == 0
                steps = {}
                if not first:
                    alone = isinstance(i, int) and i == 1
                    steps = ffn(i - 1, 2, (s_copied, 1) if alone else (s_combined, i - 1),
                                sums[1 - parity])
                for j in range(chunks):
                    if j % BATCH == 0:
                        pe.wait_ge(s_select[j // BATCH], i + 1)
                    if not first:
                        pe.wait_ge(s_rows[j], 16 * (i + 1))
                    elif j % BATCH == 0:
                        pe.wait_ge(s_row_normed, j // BATCH + 1)
                    own = first or j >= LOW and chunks == PER_PAIR
                    last = add_chunk(j, parity if own else 1 - parity,
                                     STEP * j - MARGIN + (0 if own else PAIR))
                    if j % BATCH == BATCH - 1:
                        last.then_inc(s_used[j // BATCH], 1)
                    elif j == (LOW if chunks == PER_PAIR else chunks) - 1 and not first:
                        last.then_inc(s_summed, 1)
                    if j == 2 * BATCH and chunks == PER_PAIR:
                        if not first:
                            pe.wait_ge(s_copied, i)
                        clear(1 - parity)
                    for step in steps.pop(j, []):
                        step()
                run(steps)

            with pe.If(pe.value_load(flag[0:1, 0:1], min_val=0, max_val=1)):
                with pe.Fori(0, COLS // GEN) as g:
                    for j in range(GEN):
                        pe.wait_ge(s_gen_rows[j], 16 * (g + 1))
                    pe.sem_inc(s_held["pe"], 1)
                    with pe.Fori(0, N_TILES) as t:
                        step = g * N_TILES + t + 1
                        pe.wait_ge(s_gen_sel, step)
                        for k in range(KD):
                            for j in range(GEN):
                                last = pe.matmul(agg_ps[0][:, k, 0:P],
                                                 rows[:, j, k * P:(k + 1) * P],
                                                 gen_select[:, j, :],
                                                 start=(j == 0), stop=(j == GEN - 1))
                        last.then_inc(s_gen_sum, 1)
                run(ffn(0, 2, (s_combined, 1), sums[0]))
                with pe.Fori(1, N_PAIRS) as q:
                    run(ffn(q, 2, (s_combined, q + 1), sums[0]))
                run(ffn(N_PAIRS, 1, (s_combined, N_PAIRS + 1), sums[0]))
            with pe.Else():
                clear(0)
                pair(0, 0)
                pair(1, 1)
                with pe.Fori(2, N_PAIRS, 2) as i:
                    pair(i, 0)
                    pair(i + 1, 1)
                pair(N_PAIRS, 0, LAST_CHUNKS)
                run(ffn(N_PAIRS, 1, (s_copied, N_PAIRS), sums[1][:, :, PAIR:SUMS]))

        @block.vector
        def _(dve):
            dve.memset(ends_all[:, N_CHUNKS - 1:COLS, :], N_NODES - 1).then_inc(s_pad, 1)
            dve.memset(w_all[:, N_CHUNKS - 1:COLS], 0.0).then_inc(s_pad, 1)
            dve.memset(ew2_sb[:, :, :], 0.0).then_inc(s_pad, 1)
            dve.memset(zero_l[:, :], 0.0).then_inc(s_pad, 1)
            dve.memset(zero_r[:, :], 0.0).then_inc(s_pad, 1)
            dve.memset(mix[:, :, :], 1.0).then_inc(s_pad, 1)
            dve.memset(eps[:, :], LN_EPS).then_inc(s_pad, 1)

            def stage(i, parity, n=PER_PAIR):
                if not (isinstance(i, int) and i < 2):
                    dve.wait_ge(s_used[BATCHES - 1], i - 1)
                c = bass.ds(i * PER_PAIR, n)
                if not (isinstance(i, int) and i == 0):
                    dve.tensor_copy(src_now[:, parity, 0:n], src_all[:, c])
                dve.tensor_copy(rel_now[:, parity, 0:n], rel_all[:, c])
                dve.tensor_copy(w_now[:, parity, 0:n], w_all[:, c]).then_inc(s_staged, 1)

            def selectors(i, b, parity):
                if b == 0:
                    dve.wait_ge(s_staged, i + 1)
                if not (isinstance(i, int) and i == 0):
                    dve.wait_ge(s_used[b], i)
                for j in range(b * BATCH, (b + 1) * BATCH):
                    last = dve.tensor_scalar(select[:, j, :], iota[:, 0:WINDOW],
                                             rel_now[:, parity, j:j + 1], w_now[:, parity, j:j + 1],
                                             ALU.is_equal, ALU.mult)
                last.then_inc(s_select[b], 1)

            dve.wait_ge(s_ends, 16)
            dve.tensor_copy(src_now[:, 0, :], src_all[:, 0:PER_PAIR]).then_inc(s_src, 1)

            def statistics(g):
                t0, n = groups[g]
                r = P if n == 4 else TAIL
                dve.wait_ge(s_x[g], 16)
                for t in range(t0, t0 + n):
                    last = dve.bn_stats(stats0[0:r, t, :], x_sb[0:r, t, :])
                last.then_inc(s_stats0, 1)
                dve.wait_ge(s_stats0, g + 1)
                for t in range(t0, t0 + n):
                    last = dve.bn_aggr(mv0[0:r, t, :], stats0[0:r, t, :])
                last.then_inc(s_var0, 1)

            def reciprocals(g):
                t0, n = groups[g]
                r = P if n == 4 else TAIL
                dve.wait_ge(s_std0, g + 1)
                dve.reciprocal(rstd0[0:r, t0:t0 + n], std0[0:r, t0:t0 + n]).then_inc(s_rstd0, 1)
                dve.wait_ge(s_rstd0, g + 1)
                dve.scalar_tensor_tensor(out=shift0[0:r, t0:t0 + n], in0=mv0[0:r, t0:t0 + n, 0],
                                         scalar=-1.0, in1=rstd0[0:r, t0:t0 + n],
                                         op0=ALU.mult, op1=ALU.mult).then_inc(s_shift0, 1)
                if n == 4:
                    t = t0 + 3
                    dve.tensor_scalar(xn_all[:, t, :], x_sb[:, t, :], mv0[:, t, 0:1],
                                      rstd0[:, t:t + 1], ALU.subtract,
                                      ALU.mult).then_inc(s_normed_v, 1)

            def edge_tables():
                dve.wait_ge(s_edges, 16 * 3)
                dve.wait_ge(s_const, 9)
                dve.tensor_copy(dst_f[:, :], dst_i).then_inc(s_edge, 1)
                dve.wait_ge(s_edge, 1)
                dve.tensor_tensor(rel_all[:, :], dst_f[:, :], starts[:, :], ALU.subtract).then_inc(s_edge, 1)
                dve.wait_ge(s_edge, 2)
                dve.tensor_scalar(away[:, :], rel_all[:, :], (WINDOW - 1) / 2, None,
                                  ALU.subtract).then_inc(s_edge, 1)
                dve.wait_ge(s_edge, 3)
                dve.tensor_reduce(away_max[:, :], away[:, :], AX_X, ALU.max,
                                  apply_absolute_value=True).then_inc(s_away, 1)
                dve.wait_ge(s_away_t, 1)
                dve.tensor_reduce(farthest[:, :], mid_ps[0:1, 0:P], AX_X, ALU.max).then_inc(s_away, 1)
                dve.wait_ge(s_away, 2)
                dve.tensor_scalar(flag[:, :], farthest[:, :], -1.0 if force_general else WINDOW / 2, None,
                                  ALU.is_gt).then_inc(s_flag, 1)

            statistics(0)
            for g in range(1, len(groups)):
                statistics(g)
                reciprocals(g - 1)
                if g == 2:
                    edge_tables()
            reciprocals(len(groups) - 1)
            dve.wait_ge(s_flag, 1)

            def row_statistics(b):
                c = slice(b * BATCH, (b + 1) * BATCH)
                for j in range(b * BATCH, (b + 1) * BATCH):
                    dve.wait_ge(s_rows[j], 16)
                    last = dve.bn_stats(row_stats[:, j, :], rows[:, j, :])
                last.then_inc(s_row_stats, 1)
                dve.wait_ge(s_row_stats, b + 1)
                for j in range(b * BATCH, (b + 1) * BATCH):
                    last = dve.bn_aggr(row_mv[:, j, :], row_stats[:, j, :])
                last.then_inc(s_row_var, 1)
                dve.wait_ge(s_row_std, b + 1)
                dve.reciprocal(row_rstd[:, c], row_std[:, c]).then_inc(s_row_rstd, 1)
                dve.wait_ge(s_row_rstd, b + 1)
                dve.scalar_tensor_tensor(out=row_shift[:, c], in0=row_mv[:, c, 0], scalar=-1.0,
                                         in1=row_rstd[:, c], op0=ALU.mult,
                                         op1=ALU.mult).then_inc(s_row_shift, 1)

            def add_bias(q, tiles):
                if isinstance(q, int) and q == 0:
                    dve.wait_ge(s_w, 16 * N_LOADS)
                    dve.wait_ge(s_normed, len(groups))
                T, r, _ = tile_shape(tiles)
                xq = x_sb[0:r, bass.ds(q * 2, T), :]
                dve.tensor_tensor(xq, xq, gnn_b_sb[0:r, :].unsqueeze(1).to_broadcast([r, T, D]),
                                  ALU.add).then_inc(s_resid, 1)

            def ffn(q, tiles):
                T, r, tok = tile_shape(tiles)
                first = isinstance(q, int) and q == 0
                n = q + 1
                flat = "p t d -> p (t d)"

                def residual():
                    dve.wait_ge(s_resid, n)
                    dve.wait_ge(s["lin"], n)
                    if not first:
                        dve.wait_ge(s["y"], q)
                    dve.tensor_tensor(x1[0:r, 0:T, :], by_half(tok_ps)[0:r, 0:T, :],
                                      x_sb[0:r, bass.ds(q * 2, T), :], ALU.add).then_inc(s["x1"], 1)
                    dve.wait_ge(s["x1"], n)
                    for t in range(T):
                        last = dve.bn_stats(stats[0:r, t, :], x1[0:r, t, :])
                    last.then_inc(s["stats"], 1)
                    dve.wait_ge(s["stats"], n)
                    dve.sem_inc(s_held["dve"], 1)
                    for t in range(T):
                        last = dve.bn_aggr(mv[0:r, t, :], stats[0:r, t, :])
                    last.then_inc(s["var"], 1)
                    dve.wait_ge(s["std"], n)
                    dve.reciprocal(rstd[0:r, 0:T], std[0:r, 0:T]).then_inc(s["rstd"], 1)
                    dve.wait_ge(s["rstd"], n)
                    if not first:
                        dve.wait_ge(s["turned"], q)
                    for t in range(T):
                        last = dve.tensor_scalar(xn[0:r, t, :], x1[0:r, t, :], mv[0:r, t, 0:1],
                                                 rstd[0:r, t:t + 1], ALU.subtract, ALU.mult)
                    last.then_inc(s["xn"], 1)

                def route():
                    R = slice(0, r), slice(0, T)
                    each = [r, T, E]
                    two = [r, T, E, E]

                    def wide(v):
                        return v[R].unsqueeze(2).to_broadcast(each)

                    dve.wait_ge(s["logits"], n)
                    dve.tensor_tensor(logit[R], mid_ps[0:r, LG:LG + T * E].rearrange(
                        "p (t e) -> p t e", e=E), gate_b_sb[0:r, :].unsqueeze(1).to_broadcast(each),
                        ALU.add).then_inc(s["logit"], 1)
                    dve.wait_ge(s["logit"], n)
                    dve.tensor_reduce(top[R], logit[R], AX_X, ALU.max).then_inc(s["top"], 1)
                    dve.wait_ge(s["top"], n)
                    dve.tensor_tensor(low[R], logit[R], wide(top), ALU.subtract).then_inc(s["low"], 1)
                    dve.wait_ge(s["ex"], n)
                    dve.tensor_reduce(total[R], ex[R], AX_X, ALU.add).then_inc(s["total"], 1)
                    dve.wait_ge(s["total"], n)
                    dve.reciprocal(inv[R], total[R]).then_inc(s["inv"], 1)
                    dve.wait_ge(s["inv"], n)
                    dve.tensor_tensor(gate[R], ex[R], wide(inv), ALU.mult).then_inc(s["gate"], 1)
                    dve.wait_ge(s["gate"], n)
                    dve.tensor_reduce(gtop[R], gate[R], AX_X, ALU.max).then_inc(s["gtop"], 1)
                    a = gate[R].unsqueeze(3).to_broadcast(two)
                    b = gate[R].unsqueeze(2).to_broadcast(two)
                    dve.tensor_tensor(ahead[R], b, a, ALU.is_gt).then_inc(s["ahead"], 1)
                    dve.tensor_tensor(tied[R], b, a, ALU.is_equal).then_inc(s["tied"], 1)
                    dve.wait_ge(s["tied"], n)
                    dve.tensor_tensor(glow[R], gate[R], wide(gtop), ALU.subtract).then_inc(s["glow"], 1)
                    dve.tensor_tensor(tied[R], tied[R],
                                      before[0:r, :, :].unsqueeze(1).to_broadcast(two),
                                      ALU.mult).then_inc(s["tied_before"], 1)
                    dve.wait_ge(s["tied_before"], n)
                    dve.tensor_tensor(ahead[R], ahead[R], tied[R], ALU.add).then_inc(s["order"], 1)
                    dve.wait_ge(s["order"], n)
                    dve.tensor_reduce(rank[R], ahead[R], AX_X, ALU.add).then_inc(s["rank"], 1)
                    dve.wait_ge(s["rank"], n)
                    dve.wait_ge(s["gex"], n)
                    dve.scalar_tensor_tensor(out=kept[R], in0=rank[R], scalar=1.5, in1=gex[R],
                                             op0=ALU.is_lt, op1=ALU.mult).then_inc(s["kept"], 1)
                    dve.wait_ge(s["kept"], n)
                    dve.tensor_reduce(ktotal[R], kept[R], AX_X, ALU.add).then_inc(s["ktotal"], 1)
                    dve.wait_ge(s["ktotal"], n)
                    dve.reciprocal(kinv[R], ktotal[R]).then_inc(s["kinv"], 1)
                    dve.wait_ge(s["kinv"], n)
                    if not first:
                        dve.wait_ge(s["mix_turned"], q)
                    dve.tensor_tensor(mix[0:r, 0:T, 0:E], kept[R], wide(kinv),
                                      ALU.mult).then_inc(s["mix"], 1)

                def weigh():
                    dve.wait_ge(s["mix_turned"], n)
                    if not first:
                        dve.wait_ge(s["end"], q)
                    dve.tensor_copy(mix_t[:, 0:tok], mid_ps[0:E + 1, MT:MT + tok]).then_inc(s["mixt"], 1)
                    dve.wait_ge(s["h2"], n)
                    dve.wait_ge(s["spread"], n)
                    dve.tensor_tensor(h2[:, 1:3, 0:tok], h2[:, 1:3, 0:tok],
                                      by_half(tok_ps)[:, :, 0:tok], ALU.mult).then_inc(s["mixed"], 1)

                def finish():
                    dve.wait_ge(s["end"], n)
                    if not first:
                        dve.wait_ge(s_out, 16 * q)
                    dve.tensor_tensor(y[0:r, 0:T, :], by_half(tok_ps)[0:r, 0:T, :], x1[0:r, 0:T, :],
                                      ALU.add).then_inc(s["y"], 1)

                return {"residual": residual, "route": route, "weigh": weigh, "finish": finish}

            def pair(i, parity, next_n=PER_PAIR):
                first = isinstance(i, int) and i == 0
                if first:
                    stage(1, 1)
                    for b in range(1, BATCHES):
                        selectors(0, b, 0)
                        row_statistics(b)
                    selectors(1, 0, 1)
                    selectors(1, 1, 1)
                    add_bias(0, 2)
                    return
                steps = ffn(i - 1, 2)
                stage(i + 1, 1 - parity, next_n)
                selectors(i, 2, parity)
                if not (isinstance(i, int) and i == 1):
                    combine(i - 1, 1 - parity)
                steps["residual"]()
                selectors(i, 3, parity)
                steps["route"]()
                selectors(i + 1, 0, 1 - parity)
                if next_n == PER_PAIR:
                    selectors(i + 1, 1, 1 - parity)
                steps["weigh"]()
                add_bias(i, 2)
                steps["finish"]()

            def combine(q, parity):
                dve.wait_ge(s_copied, q + 1)
                begin = sums[parity][:, :, 0:CARRY]
                dve.tensor_tensor(begin, begin, sums[1 - parity][:, :, PAIR:SUMS],
                                  ALU.add).then_inc(s_combined, 1)

            def run(steps):
                for name in ("residual", "route", "weigh", "finish"):
                    steps[name]()

            def fetch_sums(q, n=PAIR):
                if not (isinstance(q, int) and q == 0):
                    dve.wait_ge(s["lin"], q)
                add_bias(q, 2 if n == PAIR else 1)
                dve.tensor_copy(sums[0][:, :, 0:n],
                                agg_all[:, :, bass.ds(q * PAIR, n)]).then_inc(s_combined, 1)

            with dve.If(dve.value_load(flag[0:1, 0:1], min_val=0, max_val=1)):
                dve.memset(agg_all[:, :, :], 0.0).then_inc(s_gen_add, 1)
                with dve.Fori(0, COLS // GEN) as g:
                    dve.wait_ge(s_gen_add, g * N_TILES + 1)
                    c = bass.ds(g * GEN, GEN)
                    dve.tensor_copy(w_now[:, 0, 0:GEN], w_all[:, c])
                    dve.tensor_copy(rel_now[:, 0, 0:GEN], dst_f[:, c]).then_inc(s_gen_rel, 1)
                    dve.tensor_copy(src_now[:, 1, 0:GEN], src_all[:, c]).then_inc(s_gen_idx, 1)
                    with dve.Fori(0, N_TILES) as t:
                        step = g * N_TILES + t + 1
                        dve.wait_ge(s_gen_rel, g * (N_TILES + 1) + t + 1)
                        dve.wait_ge(s_gen_add, step)
                        for j in range(GEN):
                            last = dve.tensor_scalar(gen_select[:, j, :], iota[:, :],
                                                     rel_now[:, 0, j:j + 1], w_now[:, 0, j:j + 1],
                                                     ALU.is_equal, ALU.mult)
                        last.then_inc(s_gen_sel, 1)
                        dve.wait_ge(s_gen_sel, step)
                        dve.tensor_scalar(rel_now[:, 0, 0:GEN], rel_now[:, 0, 0:GEN], float(P), None,
                                          ALU.subtract).then_inc(s_gen_rel, 1)
                        dve.wait_ge(s_gen_sum, step)
                        so_far = agg_all[:, :, bass.ds(t * P, P)]
                        dve.tensor_tensor(so_far, so_far,
                                          agg_ps[0][:, :, 0:P],
                                          ALU.add).then_inc(s_gen_add, 1)
                dve.wait_ge(s_gen_add, (COLS // GEN) * N_TILES + 1)
                fetch_sums(0)
                run(ffn(0, 2))
                with dve.Fori(1, N_PAIRS) as q:
                    fetch_sums(q)
                    run(ffn(q, 2))
                fetch_sums(N_PAIRS, TAIL)
                run(ffn(N_PAIRS, 1))
            with dve.Else():
                stage(0, 0)
                selectors(0, 0, 0)
                row_statistics(0)
                pair(0, 0)
                pair(1, 1)
                with dve.Fori(2, N_PAIRS - 2, 2) as i:
                    pair(i, 0)
                    pair(i + 1, 1)
                pair(N_PAIRS - 2, 0)
                pair(N_PAIRS - 1, 1, BATCH)
                add_bias(N_PAIRS, 1)
                combine(N_PAIRS - 1, 1)
                run(ffn(N_PAIRS - 1, 2))
                run(ffn(N_PAIRS, 1))


def kernel(x, src, dst, edge_weight, L0_gnn_W, L0_gnn_b, L0_ffn_sW1, L0_ffn_sb1, L0_ffn_sW2,
           L0_ffn_sb2, L0_ffn_sW3, L0_ffn_sb3, L0_ffn_eW1, L0_ffn_eb1, L0_ffn_eW2, L0_ffn_eb2,
           L0_ffn_eW3, L0_ffn_eb3, L0_ffn_gW, L0_ffn_gb):
    import numpy as np
    import concourse.bacc as bacc
    from concourse.bass_utils import run_bass_kernel_spmd

    def chunks(a):
        a = np.asarray(a)
        whole = (N_CHUNKS - 1) * P
        return a[:whole].reshape(N_CHUNKS - 1, P).T, a[whole:].reshape(TAIL_EDGES, 1)

    def row(a):
        return np.asarray(a).reshape(1, -1)

    ew1 = np.asarray(L0_ffn_eW1).reshape(E, KD, P, P).transpose(2, 1, 0, 3)
    ew3 = np.asarray(L0_ffn_eW3).reshape(2, P, D).transpose(1, 0, 2)
    b1 = np.concatenate([np.asarray(L0_ffn_sb1).reshape(2, P), np.asarray(L0_ffn_eb1)]).T
    b2 = np.concatenate([row(L0_ffn_sb2), np.asarray(L0_ffn_eb2).reshape(2, P)]).T
    b3 = np.concatenate([np.asarray(L0_ffn_eb3), row(L0_ffn_sb3)])
    ends = [np.stack(a, axis=2) for a in zip(chunks(src), chunks(dst))]
    laid = [x, *ends, *chunks(edge_weight), np.asarray(L0_gnn_W).T, row(L0_gnn_b),
            L0_ffn_sW1, ew1, b1, L0_ffn_sW2, L0_ffn_eW2, b2, L0_ffn_sW3, ew3, b3, L0_ffn_gW,
            row(L0_ffn_gb)]
    names = ["x", "ends", "ends_tail", "wgt", "wgt_tail", "gnn_wt", "gnn_b", "sw1",
             "ew1", "b1", "sw2", "ew2", "b2", "sw3", "ew3", "b3", "gate_w", "gate_b"]
    nc = bacc.Bacc("TRN2", target_bir_lowering=False, num_devices=1)
    arrays, args = {}, []
    for name, a in zip(names, laid):
        a = np.ascontiguousarray(a)
        arrays[f"in_{name}"] = a
        args.append(nc.dram_tensor(f"in_{name}", a.shape, mybir.dt.from_np(a.dtype),
                                   kind="ExternalInput").ap())
    out = nc.dram_tensor("out", (N_NODES, D), F32, kind="ExternalOutput").ap()
    build(nc, *args, out)
    return run_bass_kernel_spmd(nc, [arrays], core_ids=[0]).results[0]["out"]
```

```python
from contextlib import ExitStack

import concourse.bass as bass
from concourse import mybir

P = 128
F32 = mybir.dt.float32
BF16 = mybir.dt.bfloat16
I32 = mybir.dt.int32
ALU = mybir.AluOpType
ACT = mybir.ActivationFunctionType
AX_X = mybir.AxisListType.X
LN_EPS = 1e-5

N_NODES, N_EDGES, D = 3125, 50000, 256
KD = D // P
N_TILES = -(-N_NODES // P)
TAIL = N_NODES - (N_TILES - 1) * P
PAIR = 2 * P
N_PAIRS = N_NODES // PAIR
N_CHUNKS = -(-N_EDGES // P)
TAIL_EDGES = N_EDGES - (N_CHUNKS - 1) * P
STEP = 8
BATCH = 8
PER_PAIR = PAIR // STEP
BATCHES = PER_PAIR // BATCH
HALF = BATCH // 2
COLS = -(-N_CHUNKS // BATCH) * BATCH
MARGIN = 44
WINDOW = STEP + 2 * MARGIN
LAST_CHUNKS = N_CHUNKS - N_PAIRS * PER_PAIR
LONE, END = N_PAIRS - 1, N_PAIRS
LOW = -(-MARGIN // STEP)
CARRY = STEP * LOW + MARGIN
SUMS = PAIR + CARRY
END_CHUNK = -(-(P + MARGIN) // STEP)
E = 4
H1 = 6
GEN = 4
assert N_EDGES == N_NODES * P // STEP and COLS % GEN == 0 and SUMS <= 512
assert LAST_CHUNKS <= BATCH and 2 * BATCH < END_CHUNK and N_TILES == 2 * N_PAIRS + 1
assert STEP * END_CHUNK + MARGIN - P <= CARRY


class WorkingSet:
    pass


def build(nc, x, src, src_tail, dst, dst_tail, wgt, wgt_tail, gnn_wt, gnn_b, sw1, ew1, b1,
          sw2, ew2, b2, sw3, ew3, b3, gate_w, gate_b, out, force_general=False):
    table = nc.dram_tensor("normalised_rows", [N_NODES, D], F32)

    with ExitStack() as ctx:
        def sb(name, shape, dt=F32):
            return ctx.enter_context(nc.sbuf_tensor(name, shape, dt))

        def bank(name):
            return ctx.enter_context(nc.psum_tensor(name, [P, 512], F32))

        def sem(name):
            return ctx.enter_context(nc.semaphore(name))

        x_sb = sb("x_sb", [P, N_TILES, D])
        xn_all = sb("xn_all", [P, N_TILES, D])
        stats0 = sb("stats0", [P, N_TILES, 6])
        mv0 = sb("mv0", [P, N_TILES, 2])
        std0 = sb("std0", [P, N_TILES])
        rstd0 = sb("rstd0", [P, N_TILES])
        row_stats = sb("row_stats", [P, PER_PAIR, 6])
        row_mv = sb("row_mv", [P, PER_PAIR, 2])
        row_std = sb("row_std", [P, PER_PAIR])
        row_rstd = sb("row_rstd", [P, PER_PAIR])
        row_shift = sb("row_shift", [P, PER_PAIR])
        shift0 = sb("shift0", [P, N_TILES])
        eps = sb("eps", [P, 1])
        src_all = sb("src_all", [P, COLS], I32)
        dst_i = sb("dst_i", [P, COLS], I32)
        dst_f = sb("dst_f", [P, COLS])
        rel_all = sb("rel_all", [P, COLS])
        w_all = sb("w_all", [P, COLS])
        starts = sb("starts", [P, COLS])
        away = sb("away", [P, COLS])
        away_max = sb("away_max", [P, 1])
        farthest = sb("farthest", [1, 1])
        flag = sb("flag", [1, 1], I32)
        src_now = sb("src_now", [P, 2, PER_PAIR], I32)
        rel_now = sb("rel_now", [P, 2, PER_PAIR])
        w_now = sb("w_now", [P, 2, PER_PAIR])
        rows = sb("rows", [P, PER_PAIR, D])
        select = sb("select", [P, PER_PAIR, WINDOW])
        ident = sb("ident", [P, P])
        iota = sb("iota", [P, P])
        before = sb("before", [P, E, E])
        owner = sb("owner", [E + 1, 2, P])
        zero_l = sb("zero_l", [1, P], BF16)
        zero_r = sb("zero_r", [1, 512], BF16)
        gnn_wt_sb = sb("gnn_wt_sb", [P, KD, D])
        gnn_b_sb = sb("gnn_b_sb", [P, D])
        sw1_sb = sb("sw1_sb", [P, KD, D])
        ew1_sb = sb("ew1_sb", [P, KD, E, P])
        b1_sb = sb("b1_sb", [P, H1])
        sw2_sb = sb("sw2_sb", [P, KD, P])
        ew2_sb = sb("ew2_sb", [P, E, P])
        b2_sb = sb("b2_sb", [P, 3])
        sw3_sb = sb("sw3_sb", [P, D])
        ew3_sb = sb("ew3_sb", [P, 2, D])
        b3_sb = sb("b3_sb", [E + 1, D])
        gate_w_sb = sb("gate_w_sb", [P, KD, E])
        gate_b_sb = sb("gate_b_sb", [P, E])
        sums = [sb(f"sums{k}", [P, KD, SUMS]) for k in range(2)]
        sets = []
        for k in range(2):
            u = WorkingSet()
            u.x1 = sb(f"x1_{k}", [P, 2, D])
            u.stats = sb(f"stats_{k}", [P, 2, 6])
            u.mv = sb(f"mv_{k}", [P, 2, 2])
            u.std = sb(f"std_{k}", [P, 2])
            u.rstd = sb(f"rstd_{k}", [P, 2])
            u.xn = sb(f"xn_{k}", [P, 2, D])
            u.xt = sb(f"xt_{k}", [P, KD, PAIR])
            u.logit = sb(f"logit_{k}", [P, 2, E])
            u.top = sb(f"top_{k}", [P, 2])
            u.low = sb(f"low_{k}", [P, 2, E])
            u.ex = sb(f"ex_{k}", [P, 2, E])
            u.total = sb(f"total_{k}", [P, 2])
            u.inv = sb(f"inv_{k}", [P, 2])
            u.gate = sb(f"gate_{k}", [P, 2, E])
            u.gtop = sb(f"gtop_{k}", [P, 2])
            u.glow = sb(f"glow_{k}", [P, 2, E])
            u.gex = sb(f"gex_{k}", [P, 2, E])
            u.ahead = sb(f"ahead_{k}", [P, 2, E, E])
            u.tied = sb(f"tied_{k}", [P, 2, E, E])
            u.rank = sb(f"rank_{k}", [P, 2, E])
            u.kept = sb(f"kept_{k}", [P, 2, E])
            u.ktotal = sb(f"ktotal_{k}", [P, 2])
            u.kinv = sb(f"kinv_{k}", [P, 2])
            u.mix = sb(f"mix_{k}", [P, 2, E + 1])
            u.mix_t = sb(f"mix_t_{k}", [E + 1, PAIR])
            u.h1 = sb(f"h1_{k}", [P, H1, PAIR])
            u.h2 = sb(f"h2_{k}", [P, 3, PAIR])
            u.y = sb(f"y_{k}", [P, 2, D])
            sets.append(u)
        agg_all = xn_all[:, :, :].rearrange("p t d -> p (t d)").rearrange("p (k n) -> p k n", k=KD)

        agg_ps = [ctx.enter_context(nc.psum_tensor(f"agg{k}_ps", [P, KD, 512], F32)) for k in range(2)]
        sets[0].tok_ps = bank("tok_ps")
        sets[0].mid_ps = bank("mid_ps")
        sets[0].hid_ps = [bank(f"hid{k}_ps") for k in range(2)]
        sets[1].tok_ps, sets[1].mid_ps = agg_ps[1][:, 0, :], agg_ps[1][:, 1, :]
        sets[1].hid_ps = [agg_ps[0][:, k, :] for k in range(2)]

        gen_select = select[:, :, :].rearrange("p j n -> p (j n)")[:, 0:GEN * P].rearrange(
            "p (j n) -> p j n", j=GEN)

        def by_half(t):
            return t[:, :].rearrange("p (k n) -> p k n", k=2)

        LG = 0
        MT = P

        s_x = [sem(f"s_x{g}") for g in range(7)]
        s_first_src = sem("s_first_src")
        s_edges = sem("s_edges")
        s_src = sem("s_src")
        s_w = sem("s_w")
        s_pad = sem("s_pad")
        s_x_pad = sem("s_x_pad")
        s_filled = sem("s_filled")
        s_const = sem("s_const")
        s_stats0 = sem("s_stats0")
        s_var0 = sem("s_var0")
        s_std0 = sem("s_std0")
        s_rstd0 = sem("s_rstd0")
        s_shift0 = sem("s_shift0")
        s_normed = sem("s_normed")
        s_normed_v = sem("s_normed_v")
        s_row_stats = sem("s_row_stats")
        s_row_var = sem("s_row_var")
        s_row_std = sem("s_row_std")
        s_row_rstd = sem("s_row_rstd")
        s_row_shift = sem("s_row_shift")
        s_row_normed = sem("s_row_normed")
        s_row_normed_v = sem("s_row_normed_v")
        s_edge = sem("s_edge")
        s_resid = sem("s_resid")
        s_table = sem("s_table")
        s_away = sem("s_away")
        s_away_t = sem("s_away_t")
        s_flag = sem("s_flag")
        s_staged = sem("s_staged")
        s_rows = [sem(f"s_rows{j}") for j in range(PER_PAIR)]
        s_select = [sem(f"s_select{b}") for b in range(BATCHES)]
        s_used = [sem(f"s_used{b}") for b in range(2 * BATCHES)]
        s_summed = sem("s_summed")
        s_copied = sem("s_copied")
        s_combined = sem("s_combined")
        steps_of_unit = (
            "lin x1 stats var std rstd xn turned xt logits logit top low ex total inv gate gtop "
            "ahead tied tied_before glow gex order rank kept ktotal kinv mix mix_turned mixt "
            "h1a h1b h1 l2 h2 spread mixed end y").split()
        s = {n: sem("ffn_" + n) for n in steps_of_unit}
        s_l1 = [sem(f"s_l1_{k}") for k in range(3)]
        s_held = {n: sem(f"s_held_{n}") for n in ("pool", "pe", "dve")}
        s_out = sem("s_out")
        s_gen_rows = [sem(f"s_gen_rows{j}") for j in range(GEN)]
        s_gen_idx = sem("s_gen_idx")
        s_gen_rel = sem("s_gen_rel")
        s_gen_sel = sem("s_gen_sel")
        s_gen_sum = sem("s_gen_sum")
        s_gen_add = sem("s_gen_add")

        groups = [(4 * g, 4) for g in range(6)] + [(N_TILES - 1, 1)]
        ROWS_AFTER = 3
        ACT_TILES = (3, 3, 3, 2, 2, 2, 1)
        ACT_ROWS = 5
        N_LOADS = 16

        block = ctx.enter_context(nc.Block())

        def unit(q):
            if isinstance(q, int) and q == LONE:
                return 2 * q, 1, P, sets[0]
            if isinstance(q, int) and q == END:
                return 2 * q - 1, 2, P + TAIL, sets[1]
            return q * 2, 2, PAIR, sets[0]

        def set_is_used(q):
            return not (isinstance(q, int) and q in (0, END))

        @block.sync
        def _(sp):
            sp.dma_start(src_now[:, 0, :], src[:, 0:PER_PAIR]).then_inc(s_first_src, 16)
            for g, (t0, n) in enumerate(groups):
                if n == 4:
                    sp.dma_start(x_sb[:, t0:t0 + n, :],
                                 x[t0 * P:(t0 + n) * P, :].rearrange("(t p) d -> p t d", p=P)
                                 ).then_inc(s_x[g], 16)
                    if g == 0:
                        sp.dma_start(dst_i[:, 0:N_CHUNKS - 1], dst).then_inc(s_edges, 16)
                    if g == 1:
                        sp.dma_start(w_all[:, 0:N_CHUNKS - 1], wgt).then_inc(s_edges, 16)
                else:
                    sp.wait_ge(s_x_pad, 1)
                    sp.dma_start(x_sb[0:TAIL, t0, :], x[t0 * P:N_NODES, :]).then_inc(s_x[g], 16)
            sp.dma_start(src_all[:, 0:N_CHUNKS - 1], src).then_inc(s_src, 16)
            for g, (t0, n) in enumerate(groups):
                sp.wait_ge(s_normed, g + 1)
                sp.wait_ge(s_normed_v, min(g + 1, 6))
                if n == 4:
                    sp.dma_start(table[t0 * P:(t0 + n) * P, :].rearrange("(t p) d -> p t d", p=P),
                                 xn_all[:, t0:t0 + n, :]).then_inc(s_table, 16)
                else:
                    sp.dma_start(table[t0 * P:N_NODES, :], xn_all[0:TAIL, t0, :]).then_inc(s_table, 16)

            def load(dst_ap, src_ap):
                sp.dma_start(dst_ap, src_ap).then_inc(s_w, 16)

            sp.wait_ge(s_pad, 4)
            load(gnn_b_sb[:, :], gnn_b.to_broadcast([P, D]))
            load(gnn_wt_sb[:, :, :], gnn_wt.rearrange("(k p) n -> p k n", p=P))
            load(gate_w_sb[:, :, :], gate_w.rearrange("(k p) n -> p k n", p=P))
            load(gate_b_sb[:, :], gate_b.to_broadcast([P, E]))
            load(sw1_sb[:, :, :], sw1.rearrange("(k p) n -> p k n", p=P))
            load(ew1_sb[:, :, :, :], ew1)
            for e in range(E):
                half = 64 * (e % 2)
                load(ew2_sb[:, e, half:half + 64], ew2[e])
            load(b1_sb[:, :], b1)
            load(sw2_sb[:, :, :], sw2.rearrange("(k p) n -> p k n", p=P))
            load(b2_sb[:, :], b2)
            load(sw3_sb[:, :], sw3)
            load(ew3_sb[:, :, :], ew3)
            load(b3_sb[:, :], b3)

            def store(q):
                tile, T, tok, u = unit(q)
                sp.wait_ge(s["y"], q + 1)
                whole = tok // P
                sp.dma_start(out[bass.ds(tile * P, whole * P), :].rearrange("(t p) d -> p t d", p=P),
                             u.y[:, 0:whole, :]).then_inc(s_out, 16)
                if whole < T:
                    sp.dma_start(out[N_NODES - TAIL:N_NODES, :],
                                 u.y[0:TAIL, whole, :]).then_inc(s_out, 16)

            with sp.Fori(0, LONE) as q:
                store(q)
            store(LONE)
            store(END)
            sp.wait_ge(s_out, 16 * (END + 2))

        @block.gpsimd
        def _(pool):
            pool.iota(starts[:, :], pattern=[[STEP, COLS]], base=-MARGIN, channel_multiplier=0,
                      allow_small_or_imprecise_dtypes=True).then_inc(s_const, 1)
            pool.iota(iota[:, :], pattern=[[1, P]], base=0, channel_multiplier=0,
                      allow_small_or_imprecise_dtypes=True).then_inc(s_const, 1)
            pool.wait_ge(s_filled, 3)
            pool.affine_select(out=ident[:, :], in_=ident[:, :], compare_op=ALU.not_equal, fill=1.0,
                               base=0, pattern=[[-1, P]], channel_multiplier=1).then_inc(s_const, 1)
            pool.affine_select(out=before[:, :, :], in_=before[:, :, :], compare_op=ALU.is_gt,
                               fill=0.0, base=0, pattern=[[1, E], [-1, E]],
                               channel_multiplier=0).then_inc(s_const, 1)
            pool.affine_select(out=owner[:, :, :], in_=owner[:, :, :], compare_op=ALU.is_ge,
                               fill=0.0, base=0, pattern=[[P, 2], [1, P]],
                               channel_multiplier=-64).then_inc(s_const, 1)
            pool.wait_ge(s_const, 5)
            pool.affine_select(out=owner[:, :, :], in_=owner[:, :, :], compare_op=ALU.is_ge,
                               fill=0.0, base=63, pattern=[[-P, 2], [-1, P]],
                               channel_multiplier=64).then_inc(s_const, 1)
            pool.wait_ge(s_first_src, 16)
            for j in range(PER_PAIR):
                pool.indirect_dma_start(
                    rows[:, j, :], None, x[:, :],
                    bass.IndirectOffsetOnAxis(ap=src_now[:, 0, j:j + 1], axis=0)
                ).then_inc(s_rows[j], 16)
            pool.wait_ge(s_table, 16 * len(groups))
            pool.wait_ge(s_flag, 1)

            def gather_pair(i, parity, chunks=PER_PAIR):
                pool.wait_ge(s_staged, i + 1)
                pool.sem_inc(s_held["pool"], 1)
                for j in range(chunks):
                    if j % HALF == 0:
                        pool.wait_ge(s_used[j // HALF], i)
                        pool.sem_inc(s_held["pool"], 1)
                    pool.indirect_dma_start(
                        rows[:, j, :], None, table[:, :],
                        bass.IndirectOffsetOnAxis(ap=src_now[:, parity, j:j + 1], axis=0)
                    ).then_inc(s_rows[j], 16)

            with pool.If(pool.value_load(flag[0:1, 0:1], min_val=0, max_val=1)):
                pool.wait_ge(s_row_normed, 1)
                pool.wait_ge(s_row_normed_v, 1)
                with pool.Fori(0, COLS // GEN) as g:
                    pool.wait_ge(s_gen_idx, g + 1)
                    pool.sem_inc(s_held["pool"], 1)
                    for j in range(GEN):
                        pool.indirect_dma_start(
                            rows[:, j, :], None, table[:, :],
                            bass.IndirectOffsetOnAxis(ap=src_now[:, 1, j:j + 1], axis=0)
                        ).then_inc(s_gen_rows[j], 16)
            with pool.Else():
                gather_pair(1, 1)
                with pool.Fori(2, N_PAIRS, 2) as i:
                    gather_pair(i, 0)
                    gather_pair(i + 1, 1)
                gather_pair(N_PAIRS, 0, LAST_CHUNKS)

        @block.scalar
        def _(act):
            last_chunk = slice(N_CHUNKS - 1, N_CHUNKS)
            act.wait_ge(s_pad, 3)
            act.dma_start(dst_i[0:TAIL_EDGES, last_chunk], dst_tail).then_inc(s_edges, 16)
            act.dma_start(w_all[0:TAIL_EDGES, last_chunk], wgt_tail).then_inc(s_edges, 16)
            act.dma_start(src_all[0:TAIL_EDGES, last_chunk], src_tail).then_inc(s_src, 16)

            act.wait_ge(s_pad, 8)

            def normalise_rows(b):
                c = slice(b * BATCH, (b + 1) * BATCH)
                act.wait_ge(s_row_var, b + 1)
                act.activation(row_std[:, c], row_mv[:, c, 1], ACT.Sqrt,
                               bias=eps[:, :]).then_inc(s_row_std, 1)
                act.wait_ge(s_row_shift, b + 1)
                for j in range(b * BATCH, b * BATCH + ACT_ROWS):
                    last = act.activation(rows[:, j, :], rows[:, j, :], ACT.Identity,
                                          bias=row_shift[:, j:j + 1], scale=row_rstd[:, j:j + 1])
                last.then_inc(s_row_normed, 1)

            for g, (t0, n) in enumerate(groups):
                r = P if n == 4 else TAIL
                act.wait_ge(s_var0, g + 1)
                act.activation(std0[0:r, t0:t0 + n], mv0[0:r, t0:t0 + n, 1], ACT.Sqrt,
                               bias=eps[0:r, :]).then_inc(s_std0, 1)
                act.wait_ge(s_shift0, g + 1)
                for t in range(t0, t0 + ACT_TILES[g]):
                    last = act.activation(xn_all[0:r, t, :], x_sb[0:r, t, :], ACT.Identity,
                                          bias=shift0[0:r, t:t + 1], scale=rstd0[0:r, t:t + 1])
                last.then_inc(s_normed, 1)
                if g == ROWS_AFTER - 1:
                    normalise_rows(0)

            def copy_sums(q, parity):
                act.wait_ge(s_summed, q + 1)
                if not (isinstance(q, int) and q == 0):
                    act.wait_ge(s["lin"], q)
                n = PAIR if isinstance(q, int) and q == END else SUMS
                act.activation(sums[parity][:, :, 0:n], agg_ps[parity][:, :, 0:n],
                               ACT.Copy).then_inc(s_copied, 1)

            def ffn_steps(q):
                _, T, tok, u = unit(q)
                used = set_is_used(q)
                n = q + 1

                def deviation():
                    act.wait_ge(s["var"], n)
                    act.activation(u.std[:, 0:T], u.mv[:, 0:T, 1], ACT.Sqrt,
                                   bias=eps[:, :]).then_inc(s["std"], 1)

                def copy_turned():
                    act.wait_ge(s["turned"], n)
                    if used:
                        act.wait_ge(s_l1[2], q)
                    act.activation(u.xt[:, :, 0:tok], by_half(u.mid_ps)[:, :, 0:tok],
                                   ACT.Copy).then_inc(s["xt"], 1)

                def gates_exp():
                    act.wait_ge(s["low"], n)
                    act.activation(u.ex[:, 0:T, :], u.low[:, 0:T, :], ACT.Exp).then_inc(s["ex"], 1)

                def weights_exp():
                    act.wait_ge(s["glow"], n)
                    act.activation(u.gex[:, 0:T, :], u.glow[:, 0:T, :], ACT.Exp).then_inc(s["gex"], 1)

                def relu1(k):
                    if k == 0 and used:
                        act.wait_ge(s["l2"], q)
                    act.wait_ge(s_l1[k], n)
                    for m in (2 * k, 2 * k + 1):
                        last = act.activation(u.h1[:, m, 0:tok],
                                              by_half(u.hid_ps[k % 2])[:, m % 2, 0:tok],
                                              ACT.Relu, bias=b1_sb[:, m:m + 1])
                    last.then_inc(s[("h1a", "h1b", "h1")[k]], 1)

                def relu2():
                    act.wait_ge(s["l2"], n)
                    if used:
                        act.wait_ge(s["end"], q)
                    act.activation(u.h2[:, 0, 0:tok], u.hid_ps[1][:, 0:tok], ACT.Relu,
                                   bias=b2_sb[:, 0:1])
                    for k in range(2):
                        last = act.activation(u.h2[:, 1 + k, 0:tok],
                                              by_half(u.hid_ps[0])[:, k, 0:tok],
                                              ACT.Relu, bias=b2_sb[:, 1 + k:2 + k])
                    last.then_inc(s["h2"], 1)

                return (deviation, copy_turned, gates_exp, lambda: relu1(0), weights_exp,
                        lambda: relu1(1), lambda: relu1(2), relu2)

            def ffn(q):
                for step in ffn_steps(q):
                    step()

            act.wait_ge(s_flag, 1)
            with act.If(act.value_load(flag[0:1, 0:1], min_val=0, max_val=1)):
                ffn(0)
                with act.Fori(1, LONE) as q:
                    ffn(q)
                ffn(LONE)
                ffn(END)
            with act.Else():
                for b in range(1, BATCHES):
                    normalise_rows(b)
                copy_sums(0, 0)
                ffn(0)
                with act.Fori(1, LONE - 1, 2) as q:
                    copy_sums(q, 1)
                    ffn(q)
                    copy_sums(q + 1, 0)
                    ffn(q + 1)
                copy_sums(LONE, 1)
                std_a, xt_a, ex_a, h1a_a, gex_a, h1b_a, h1_a, h2_a = ffn_steps(LONE)
                std_b, xt_b, ex_b, h1a_b, gex_b, h1b_b, h1_b, h2_b = ffn_steps(END)
                for step in (std_a, lambda: copy_sums(END, 0), xt_a, std_b, h1a_a, ex_a, h1b_a,
                             h1_a, xt_b, gex_a, h2_a, ex_b, h1a_b, gex_b, h1b_b, h1_b, h2_b):
                    step()

        @block.tensor
        def _(pe):
            pe.wait_ge(s_const, 6)
            pe.wait_ge(s_away, 1)
            pe.transpose(sets[0].mid_ps[0:1, 0:P], away_max[:, :], ident[:, :]).then_inc(s_away_t, 1)
            pe.wait_ge(s_flag, 1)
            pe.wait_ge(s_pad, 8)

            def clear(parity):
                for k in range(KD):
                    pe.matmul(agg_ps[parity][:, k, 0:SUMS], zero_l[:, :], zero_r[:, 0:SUMS],
                              start=True, stop=False, skip_group_check=True)

            def add_chunk(j, parity, first_node):
                skip = max(-first_node, 0)
                for k in range(KD):
                    last = pe.matmul(agg_ps[parity][:, k, first_node + skip:first_node + WINDOW],
                                     rows[:, j, k * P:(k + 1) * P], select[:, j, skip:],
                                     start=False, stop=False, skip_group_check=True)
                return last

            def ffn(q, ready, sums_q):
                tile, T, tok, u = unit(q)
                used = set_is_used(q)
                n = q + 1
                rows_of = [min(tok - t * P, P) for t in range(T)]

                def linear():
                    if isinstance(q, int) and q == 0:
                        pe.wait_ge(s_w, 16 * N_LOADS)
                    pe.wait_ge(ready[0], ready[1])
                    if used:
                        pe.wait_ge(s["y"], q)
                    for t in range(T):
                        for k in range(KD):
                            last = pe.matmul(u.tok_ps[:, t * D:(t + 1) * D],
                                             sums_q[:, k, t * P:(t + 1) * P],
                                             gnn_wt_sb[:, k, :], start=(k == 0), stop=(k == KD - 1))
                    last.then_inc(s["lin"], 1)

                def turn():
                    pe.wait_ge(s["xn"], n)
                    if used:
                        pe.wait_ge(s["mixt"], q)
                    for t in range(T):
                        for k in range(KD):
                            last = pe.transpose(u.mid_ps[:, k * PAIR + t * P:k * PAIR + (t + 1) * P],
                                                u.xn[:, t, k * P:(k + 1) * P], ident[:, :])
                    last.then_inc(s["turned"], 1)

                def logits():
                    pe.wait_ge(s["xt"], n)
                    for t in range(T):
                        for k in range(KD):
                            last = pe.matmul(u.mid_ps[0:rows_of[t], LG + t * E:LG + (t + 1) * E],
                                             u.xt[:, k, t * P:t * P + rows_of[t]], gate_w_sb[:, k, :],
                                             start=(k == 0), stop=(k == KD - 1))
                    last.then_inc(s["logits"], 1)

                def layer1(b):
                    if b == 2:
                        pe.wait_ge(s["h1a"], n)
                    elif used:
                        pe.wait_ge(s["h2"], q)
                    for m in (2 * b, 2 * b + 1):
                        for k in range(KD):
                            w = sw1_sb[:, k, m * P:(m + 1) * P] if m < 2 else ew1_sb[:, k, m - 2, :]
                            last = pe.matmul(by_half(u.hid_ps[b % 2])[:, m % 2, 0:tok],
                                             w, u.xt[:, k, 0:tok],
                                             start=(k == 0), stop=(k == KD - 1))
                    last.then_inc(s_l1[b], 1)

                def layer2():
                    pe.wait_ge(s["h1"], n)
                    for k in range(KD):
                        pe.matmul(u.hid_ps[1][:, 0:tok], sw2_sb[:, k, :], u.h1[:, k, 0:tok],
                                  start=(k == 0), stop=(k == KD - 1))
                    for e in range(E):
                        last = pe.matmul(by_half(u.hid_ps[0])[:, e // 2, 0:tok], ew2_sb[:, e, :],
                                         u.h1[:, 2 + e, 0:tok], start=(e % 2 == 0), stop=(e % 2 == 1))
                    last.then_inc(s["l2"], 1)

                def turn_gates():
                    pe.wait_ge(s["mix"], n)
                    for t in range(T):
                        last = pe.transpose(u.mid_ps[0:E + 1, MT + t * P:MT + (t + 1) * P],
                                            u.mix[:, t, :], ident[:, :])
                    last.then_inc(s["mix_turned"], 1)

                def spread():
                    pe.wait_ge(s["mixt"], n)
                    pe.wait_ge(s["x1"], n)
                    for k in range(2):
                        last = pe.matmul(by_half(u.tok_ps)[:, k, 0:tok], owner[:, k, :],
                                         u.mix_t[:, 0:tok], start=True, stop=True)
                    last.then_inc(s["spread"], 1)

                def layer3():
                    pe.wait_ge(s["mixed"], n)
                    for t in range(T):
                        o = u.tok_ps[0:rows_of[t], t * D:(t + 1) * D]
                        c = slice(t * P, t * P + rows_of[t])
                        pe.matmul(o, u.h2[:, 0, c], sw3_sb[:, :], start=True, stop=False)
                        for k in range(2):
                            pe.matmul(o, u.h2[:, 1 + k, c], ew3_sb[:, k, :], start=False, stop=False)
                        last = pe.matmul(o, u.mix_t[:, c], b3_sb[:, :], start=False, stop=True)
                    last.then_inc(s["end"], 1)

                return (linear, turn, logits, lambda: layer1(0), lambda: layer1(1),
                        lambda: layer1(2), turn_gates, layer2, spread, layer3)

            def pair(i, parity):
                first = isinstance(i, int) and i == 0
                last_pair = isinstance(i, int) and i == LONE
                steps = {}
                if not first:
                    alone = isinstance(i, int) and i == 1
                    lin, trn, lgt, l1a, l1b, l1c, tgt, l2, spr, l3 = ffn(
                        i - 1, (s_copied, 1) if alone else (s_combined, i - 1), sums[1 - parity])
                    if last_pair:
                        steps = {8: [lin], 12: [trn], 15: [lgt, l1a], 16: [l1b], 17: [l1c],
                                 21: [tgt, l2], 23: [spr], 27: [l3]}
                    else:
                        steps = {9: [lin], 14: [trn], 17: [lgt, l1a], 18: [l1b], 19: [l1c],
                                 22: [l2], 23: [tgt], 25: [spr], 29: [l3]}
                for j in range(PER_PAIR):
                    if j % BATCH == 0:
                        pe.wait_ge(s_select[j // BATCH], i + 1)
                    if not first:
                        pe.wait_ge(s_rows[j], 16 * (i + 1))
                    elif j % BATCH == 0:
                        pe.wait_ge(s_row_normed, j // BATCH + 1)
                        pe.wait_ge(s_row_normed_v, j // BATCH + 1)
                    begin = STEP * j - MARGIN
                    if not first and j < LOW:
                        last = add_chunk(j, 1 - parity, begin + PAIR)
                    elif last_pair and j >= END_CHUNK:
                        last = add_chunk(j, 1 - parity, begin - P)
                    else:
                        last = add_chunk(j, parity, begin)
                    if j % HALF == HALF - 1:
                        last.then_inc(s_used[j // HALF], 1)
                    elif j == LOW - 1 and not first or j == END_CHUNK - 1 and last_pair:
                        last.then_inc(s_summed, 1)
                    if j == 2 * BATCH:
                        if not first:
                            pe.wait_ge(s_copied, i)
                        clear(1 - parity)
                    for step in steps.get(j, []):
                        step()

            def last_chunks(steps):
                pe.wait_ge(s_select[0], END + 1)
                for j in range(LAST_CHUNKS):
                    for step in steps.get(j, []):
                        step()
                    pe.wait_ge(s_rows[j], 16 * (END + 1))
                    last = add_chunk(j, 0, STEP * j - MARGIN + P)
                last.then_inc(s_summed, 1)

            with pe.If(pe.value_load(flag[0:1, 0:1], min_val=0, max_val=1)):
                with pe.Fori(0, COLS // GEN) as g:
                    for j in range(GEN):
                        pe.wait_ge(s_gen_rows[j], 16 * (g + 1))
                    pe.sem_inc(s_held["pe"], 1)
                    with pe.Fori(0, N_TILES) as t:
                        step = g * N_TILES + t + 1
                        pe.wait_ge(s_gen_sel, step)
                        for k in range(KD):
                            for j in range(GEN):
                                last = pe.matmul(agg_ps[0][:, k, 0:P],
                                                 rows[:, j, k * P:(k + 1) * P],
                                                 gen_select[:, j, :],
                                                 start=(j == 0), stop=(j == GEN - 1))
                        last.then_inc(s_gen_sum, 1)

                def run(q):
                    for step in ffn(q, (s_combined, q + 1), sums[0]):
                        step()

                run(0)
                with pe.Fori(1, LONE) as q:
                    run(q)
                run(LONE)
                run(END)
            with pe.Else():
                clear(0)
                pair(0, 0)
                pair(1, 1)
                with pe.Fori(2, LONE - 1, 2) as i:
                    pair(i, 0)
                    pair(i + 1, 1)
                pair(LONE - 1, 0)
                pair(LONE, 1)
                lin_a, trn_a, lgt_a, l1a_a, l1b_a, l1c_a, tgt_a, l2_a, spr_a, l3_a = ffn(
                    LONE, (s_combined, LONE), sums[1])
                lin_b, trn_b, lgt_b, l1a_b, l1b_b, l1c_b, tgt_b, l2_b, spr_b, l3_b = ffn(
                    END, (s_combined, END), sums[0])
                last_chunks({0: [lin_a], 6: [trn_a]})
                for step in (lin_b, lgt_a, l1a_a, l1b_a, l1c_a, trn_b, l2_a, lgt_b, l1a_b, tgt_a,
                             l1b_b, spr_a, l1c_b, tgt_b, l2_b, spr_b, l3_a, l3_b):
                    step()

        @block.vector
        def _(dve):
            dve.memset(ident[:, :], 0.0).then_inc(s_filled, 1)
            dve.memset(before[:, :, :], 1.0).then_inc(s_filled, 1)
            dve.memset(owner[:, :, :], 1.0).then_inc(s_filled, 1)
            dve.memset(dst_i[:, N_CHUNKS - 1:COLS], N_NODES - 1).then_inc(s_pad, 1)
            dve.memset(src_all[:, N_CHUNKS - 1:COLS], N_NODES - 1).then_inc(s_pad, 1)
            dve.memset(w_all[:, N_CHUNKS - 1:COLS], 0.0).then_inc(s_pad, 1)
            dve.memset(x_sb[:, N_TILES - 1, :], 0.0).then_inc(s_x_pad, 1)
            dve.memset(ew2_sb[:, :, :], 0.0).then_inc(s_pad, 1)
            dve.memset(zero_l[:, :], 0.0).then_inc(s_pad, 1)
            dve.memset(zero_r[:, :], 0.0).then_inc(s_pad, 1)
            for u in sets:
                last = dve.memset(u.mix[:, :, :], 1.0)
            last.then_inc(s_pad, 1)
            dve.memset(eps[:, :], LN_EPS).then_inc(s_pad, 1)

            def stage(i, parity, n=PER_PAIR):
                if not (isinstance(i, int) and i < 2):
                    dve.wait_ge(s_used[-1], i - 1)
                c = bass.ds(i * PER_PAIR, n)
                if not (isinstance(i, int) and i == 0):
                    dve.tensor_copy(src_now[:, parity, 0:n], src_all[:, c])
                dve.tensor_copy(rel_now[:, parity, 0:n], rel_all[:, c])
                dve.tensor_copy(w_now[:, parity, 0:n], w_all[:, c]).then_inc(s_staged, 1)

            def selectors(i, b, parity):
                if b == 0:
                    dve.wait_ge(s_staged, i + 1)
                if not (isinstance(i, int) and i == 0):
                    dve.wait_ge(s_used[2 * b + 1], i)
                for j in range(b * BATCH, (b + 1) * BATCH):
                    last = dve.tensor_scalar(select[:, j, :], iota[:, 0:WINDOW],
                                             rel_now[:, parity, j:j + 1], w_now[:, parity, j:j + 1],
                                             ALU.is_equal, ALU.mult)
                last.then_inc(s_select[b], 1)

            def statistics(g):
                t0, n = groups[g]
                r = P if n == 4 else TAIL
                dve.wait_ge(s_x[g], 16)
                for t in range(t0, t0 + n):
                    last = dve.bn_stats(stats0[0:r, t, :], x_sb[0:r, t, :])
                last.then_inc(s_stats0, 1)
                dve.wait_ge(s_stats0, g + 1)
                for t in range(t0, t0 + n):
                    last = dve.bn_aggr(mv0[0:r, t, :], stats0[0:r, t, :])
                last.then_inc(s_var0, 1)

            def reciprocals(g):
                t0, n = groups[g]
                r = P if n == 4 else TAIL
                dve.wait_ge(s_std0, g + 1)
                dve.reciprocal(rstd0[0:r, t0:t0 + n], std0[0:r, t0:t0 + n]).then_inc(s_rstd0, 1)
                dve.wait_ge(s_rstd0, g + 1)
                dve.scalar_tensor_tensor(out=shift0[0:r, t0:t0 + n], in0=mv0[0:r, t0:t0 + n, 0],
                                         scalar=-1.0, in1=rstd0[0:r, t0:t0 + n],
                                         op0=ALU.mult, op1=ALU.mult).then_inc(s_shift0, 1)
                for t in range(t0 + ACT_TILES[g], t0 + n):
                    last = dve.tensor_scalar(xn_all[:, t, :], x_sb[:, t, :], mv0[:, t, 0:1],
                                             rstd0[:, t:t + 1], ALU.subtract, ALU.mult)
                if n > ACT_TILES[g]:
                    last.then_inc(s_normed_v, 1)

            def edge_tables():
                dve.wait_ge(s_edges, 16 * 4)
                dve.wait_ge(s_const, 6)
                dve.tensor_copy(dst_f[:, :], dst_i[:, :]).then_inc(s_edge, 1)
                dve.wait_ge(s_edge, 1)
                dve.tensor_tensor(rel_all[:, :], dst_f[:, :], starts[:, :],
                                  ALU.subtract).then_inc(s_edge, 1)
                dve.wait_ge(s_edge, 2)
                dve.tensor_scalar(away[:, :], rel_all[:, :], (WINDOW - 1) / 2, None,
                                  ALU.subtract).then_inc(s_edge, 1)
                dve.wait_ge(s_edge, 3)
                dve.tensor_reduce(away_max[:, :], away[:, :], AX_X, ALU.max,
                                  apply_absolute_value=True).then_inc(s_away, 1)

            def choose_path():
                dve.wait_ge(s_away_t, 1)
                dve.tensor_reduce(farthest[:, :], sets[0].mid_ps[0:1, 0:P], AX_X,
                                  ALU.max).then_inc(s_away, 1)
                dve.wait_ge(s_away, 2)
                dve.tensor_scalar(flag[:, :], farthest[:, :], -1.0 if force_general else WINDOW / 2, None,
                                  ALU.is_gt).then_inc(s_flag, 1)

            def row_statistics(b):
                c = slice(b * BATCH, (b + 1) * BATCH)
                for j in range(b * BATCH, (b + 1) * BATCH):
                    dve.wait_ge(s_rows[j], 16)
                    last = dve.bn_stats(row_stats[:, j, :], rows[:, j, :])
                last.then_inc(s_row_stats, 1)
                dve.wait_ge(s_row_stats, b + 1)
                for j in range(b * BATCH, (b + 1) * BATCH):
                    last = dve.bn_aggr(row_mv[:, j, :], row_stats[:, j, :])
                last.then_inc(s_row_var, 1)
                dve.wait_ge(s_row_std, b + 1)
                dve.reciprocal(row_rstd[:, c], row_std[:, c]).then_inc(s_row_rstd, 1)
                dve.wait_ge(s_row_rstd, b + 1)
                dve.scalar_tensor_tensor(out=row_shift[:, c], in0=row_mv[:, c, 0], scalar=-1.0,
                                         in1=row_rstd[:, c], op0=ALU.mult,
                                         op1=ALU.mult).then_inc(s_row_shift, 1)
                for j in range(b * BATCH + ACT_ROWS, (b + 1) * BATCH):
                    last = dve.tensor_scalar(rows[:, j, :], rows[:, j, :], row_mv[:, j, 0:1],
                                             row_rstd[:, j:j + 1], ALU.subtract, ALU.mult)
                last.then_inc(s_row_normed_v, 1)

            statistics(0)
            for g in range(1, len(groups)):
                if g == 2:
                    edge_tables()
                statistics(g)
                reciprocals(g - 1)
                if g == ROWS_AFTER:
                    row_statistics(0)
                    choose_path()
                    stage(0, 0)
                    selectors(0, 0, 0)
            reciprocals(len(groups) - 1)
            dve.wait_ge(s_src, 16 * 2)
            dve.wait_ge(s_flag, 1)

            def add_bias(q):
                if isinstance(q, int) and q == 0:
                    dve.wait_ge(s_w, 16 * N_LOADS)
                    dve.wait_ge(s_normed, len(groups))
                tile, T, _, _ = unit(q)
                xq = x_sb[:, bass.ds(tile, T), :]
                dve.tensor_tensor(xq, xq, gnn_b_sb[:, :].unsqueeze(1).to_broadcast([P, T, D]),
                                  ALU.add).then_inc(s_resid, 1)

            def ffn(q):
                tile, T, tok, u = unit(q)
                used = set_is_used(q)
                n = q + 1

                def residual():
                    dve.wait_ge(s_resid, n)
                    dve.wait_ge(s["lin"], n)
                    if used:
                        dve.wait_ge(s["y"], q)
                    dve.tensor_tensor(u.x1[:, 0:T, :], by_half(u.tok_ps)[:, 0:T, :],
                                      x_sb[:, bass.ds(tile, T), :], ALU.add).then_inc(s["x1"], 1)
                    dve.wait_ge(s["x1"], n)
                    for t in range(T):
                        last = dve.bn_stats(u.stats[:, t, :], u.x1[:, t, :])
                    last.then_inc(s["stats"], 1)
                    dve.wait_ge(s["stats"], n)
                    dve.sem_inc(s_held["dve"], 1)
                    for t in range(T):
                        last = dve.bn_aggr(u.mv[:, t, :], u.stats[:, t, :])
                    last.then_inc(s["var"], 1)
                    dve.wait_ge(s["std"], n)
                    dve.reciprocal(u.rstd[:, 0:T], u.std[:, 0:T]).then_inc(s["rstd"], 1)
                    dve.wait_ge(s["rstd"], n)
                    if used:
                        dve.wait_ge(s["turned"], q)
                    for t in range(T):
                        last = dve.tensor_scalar(u.xn[:, t, :], u.x1[:, t, :], u.mv[:, t, 0:1],
                                                 u.rstd[:, t:t + 1], ALU.subtract, ALU.mult)
                    last.then_inc(s["xn"], 1)

                def route():
                    R = slice(0, P), slice(0, T)
                    each = [P, T, E]
                    two = [P, T, E, E]

                    def wide(v):
                        return v[R].unsqueeze(2).to_broadcast(each)

                    dve.wait_ge(s["logits"], n)
                    dve.tensor_tensor(u.logit[R], u.mid_ps[:, LG:LG + T * E].rearrange(
                        "p (t e) -> p t e", e=E), gate_b_sb[:, :].unsqueeze(1).to_broadcast(each),
                        ALU.add).then_inc(s["logit"], 1)
                    dve.wait_ge(s["logit"], n)
                    dve.tensor_reduce(u.top[R], u.logit[R], AX_X, ALU.max).then_inc(s["top"], 1)
                    dve.wait_ge(s["top"], n)
                    dve.tensor_tensor(u.low[R], u.logit[R], wide(u.top),
                                      ALU.subtract).then_inc(s["low"], 1)
                    dve.wait_ge(s["ex"], n)
                    dve.tensor_reduce(u.total[R], u.ex[R], AX_X, ALU.add).then_inc(s["total"], 1)
                    dve.wait_ge(s["total"], n)
                    dve.reciprocal(u.inv[R], u.total[R]).then_inc(s["inv"], 1)
                    dve.wait_ge(s["inv"], n)
                    dve.tensor_tensor(u.gate[R], u.ex[R], wide(u.inv), ALU.mult).then_inc(s["gate"], 1)
                    dve.wait_ge(s["gate"], n)
                    dve.tensor_reduce(u.gtop[R], u.gate[R], AX_X, ALU.max).then_inc(s["gtop"], 1)
                    a = u.gate[R].unsqueeze(3).to_broadcast(two)
                    b = u.gate[R].unsqueeze(2).to_broadcast(two)
                    dve.tensor_tensor(u.ahead[R], b, a, ALU.is_gt).then_inc(s["ahead"], 1)
                    dve.tensor_tensor(u.tied[R], b, a, ALU.is_equal).then_inc(s["tied"], 1)
                    dve.wait_ge(s["tied"], n)
                    dve.tensor_tensor(u.glow[R], u.gate[R], wide(u.gtop),
                                      ALU.subtract).then_inc(s["glow"], 1)
                    dve.tensor_tensor(u.tied[R], u.tied[R],
                                      before[:, :, :].unsqueeze(1).to_broadcast(two),
                                      ALU.mult).then_inc(s["tied_before"], 1)
                    dve.wait_ge(s["tied_before"], n)
                    dve.tensor_tensor(u.ahead[R], u.ahead[R], u.tied[R],
                                      ALU.add).then_inc(s["order"], 1)
                    dve.wait_ge(s["order"], n)
                    dve.tensor_reduce(u.rank[R], u.ahead[R], AX_X, ALU.add).then_inc(s["rank"], 1)
                    dve.wait_ge(s["rank"], n)
                    dve.wait_ge(s["gex"], n)
                    dve.scalar_tensor_tensor(out=u.kept[R], in0=u.rank[R], scalar=1.5, in1=u.gex[R],
                                             op0=ALU.is_lt, op1=ALU.mult).then_inc(s["kept"], 1)
                    dve.wait_ge(s["kept"], n)
                    dve.tensor_reduce(u.ktotal[R], u.kept[R], AX_X, ALU.add).then_inc(s["ktotal"], 1)
                    dve.wait_ge(s["ktotal"], n)
                    dve.reciprocal(u.kinv[R], u.ktotal[R]).then_inc(s["kinv"], 1)
                    dve.wait_ge(s["kinv"], n)
                    if used:
                        dve.wait_ge(s["mix_turned"], q)
                    dve.tensor_tensor(u.mix[:, 0:T, 0:E], u.kept[R], wide(u.kinv),
                                      ALU.mult).then_inc(s["mix"], 1)

                def keep_turned():
                    dve.wait_ge(s["mix_turned"], n)
                    if used:
                        dve.wait_ge(s["end"], q)
                    dve.tensor_copy(u.mix_t[:, 0:tok], u.mid_ps[0:E + 1, MT:MT + tok]
                                    ).then_inc(s["mixt"], 1)

                def weigh():
                    dve.wait_ge(s["h2"], n)
                    dve.wait_ge(s["spread"], n)
                    dve.tensor_tensor(u.h2[:, 1:3, 0:tok], u.h2[:, 1:3, 0:tok],
                                      by_half(u.tok_ps)[:, :, 0:tok], ALU.mult).then_inc(s["mixed"], 1)

                def finish():
                    dve.wait_ge(s["end"], n)
                    if used:
                        dve.wait_ge(s_out, 16 * q)
                    dve.tensor_tensor(u.y[:, 0:T, :], by_half(u.tok_ps)[:, 0:T, :], u.x1[:, 0:T, :],
                                      ALU.add).then_inc(s["y"], 1)

                return residual, route, keep_turned, weigh, finish

            def pair(i, parity, next_n=PER_PAIR):
                first = isinstance(i, int) and i == 0
                if first:
                    stage(1, 1)
                    for b in range(1, BATCHES):
                        row_statistics(b)
                        selectors(0, b, 0)
                    selectors(1, 0, 1)
                    selectors(1, 1, 1)
                    add_bias(0)
                    return
                residual, route, keep_turned, weigh, finish = ffn(i - 1)
                stage(i + 1, 1 - parity, next_n)
                selectors(i, 2, parity)
                if not (isinstance(i, int) and i == 1):
                    combine(i - 1, 1 - parity)
                residual()
                selectors(i, 3, parity)
                route()
                selectors(i + 1, 0, 1 - parity)
                keep_turned()
                if next_n == PER_PAIR:
                    selectors(i + 1, 1, 1 - parity)
                weigh()
                add_bias(i)
                finish()

            def combine(q, parity):
                dve.wait_ge(s_copied, q + 1)
                begin = sums[parity][:, :, 0:CARRY]
                above = P if isinstance(q, int) and q == END else PAIR
                dve.tensor_tensor(begin, begin, sums[1 - parity][:, :, above:above + CARRY],
                                  ALU.add).then_inc(s_combined, 1)

            def fetch_sums(q):
                if not (isinstance(q, int) and q == 0):
                    dve.wait_ge(s["lin"], q)
                add_bias(q)
                tile, T, _, _ = unit(q)
                dve.tensor_copy(sums[0][:, :, 0:T * P],
                                agg_all[:, :, bass.ds(tile * P, T * P)]).then_inc(s_combined, 1)

            def run(q):
                fetch_sums(q)
                for step in ffn(q):
                    step()

            with dve.If(dve.value_load(flag[0:1, 0:1], min_val=0, max_val=1)):
                dve.wait_ge(s_table, 16 * len(groups))
                dve.memset(agg_all[:, :, :], 0.0).then_inc(s_gen_add, 1)
                dve.wait_ge(s_select[0], 1)
                with dve.Fori(0, COLS // GEN) as g:
                    dve.wait_ge(s_gen_add, g * N_TILES + 1)
                    c = bass.ds(g * GEN, GEN)
                    dve.tensor_copy(w_now[:, 0, 0:GEN], w_all[:, c])
                    dve.tensor_copy(rel_now[:, 0, 0:GEN], dst_f[:, c]).then_inc(s_gen_rel, 1)
                    dve.tensor_copy(src_now[:, 1, 0:GEN], src_all[:, c]).then_inc(s_gen_idx, 1)
                    with dve.Fori(0, N_TILES) as t:
                        step = g * N_TILES + t + 1
                        dve.wait_ge(s_gen_rel, g * (N_TILES + 1) + t + 1)
                        dve.wait_ge(s_gen_add, step)
                        for j in range(GEN):
                            last = dve.tensor_scalar(gen_select[:, j, :], iota[:, :],
                                                     rel_now[:, 0, j:j + 1], w_now[:, 0, j:j + 1],
                                                     ALU.is_equal, ALU.mult)
                        last.then_inc(s_gen_sel, 1)
                        dve.wait_ge(s_gen_sel, step)
                        dve.tensor_scalar(rel_now[:, 0, 0:GEN], rel_now[:, 0, 0:GEN], float(P), None,
                                          ALU.subtract).then_inc(s_gen_rel, 1)
                        dve.wait_ge(s_gen_sum, step)
                        so_far = agg_all[:, :, bass.ds(t * P, P)]
                        dve.tensor_tensor(so_far, so_far,
                                          agg_ps[0][:, :, 0:P],
                                          ALU.add).then_inc(s_gen_add, 1)
                dve.wait_ge(s_gen_add, (COLS // GEN) * N_TILES + 1)
                run(0)
                with dve.Fori(1, LONE) as q:
                    run(q)
                run(LONE)
                run(END)
            with dve.Else():
                pair(0, 0)
                pair(1, 1)
                with dve.Fori(2, LONE - 1, 2) as i:
                    pair(i, 0)
                    pair(i + 1, 1)
                pair(LONE - 1, 0)
                pair(LONE, 1, BATCH)
                residual_a, route_a, turned_a, weigh_a, finish_a = ffn(LONE)
                residual_b, route_b, turned_b, weigh_b, finish_b = ffn(END)
                combine(LONE, 1)
                add_bias(END)
                for step in (residual_a, lambda: combine(END, 0), residual_b, route_a, turned_a,
                             route_b, weigh_a, turned_b, weigh_b, finish_a, finish_b):
                    step()



def kernel(x, src, dst, edge_weight, L0_gnn_W, L0_gnn_b, L0_ffn_sW1, L0_ffn_sb1, L0_ffn_sW2,
           L0_ffn_sb2, L0_ffn_sW3, L0_ffn_sb3, L0_ffn_eW1, L0_ffn_eb1, L0_ffn_eW2, L0_ffn_eb2,
           L0_ffn_eW3, L0_ffn_eb3, L0_ffn_gW, L0_ffn_gb):
    import numpy as np
    import concourse.bacc as bacc
    from concourse.bass_utils import run_bass_kernel_spmd

    def chunks(a):
        a = np.asarray(a)
        whole = (N_CHUNKS - 1) * P
        return a[:whole].reshape(N_CHUNKS - 1, P).T, a[whole:].reshape(TAIL_EDGES, 1)

    def row(a):
        return np.asarray(a).reshape(1, -1)

    ew1 = np.asarray(L0_ffn_eW1).reshape(E, KD, P, P).transpose(2, 1, 0, 3)
    ew3 = np.asarray(L0_ffn_eW3).reshape(2, P, D).transpose(1, 0, 2)
    b1 = np.concatenate([np.asarray(L0_ffn_sb1).reshape(2, P), np.asarray(L0_ffn_eb1)]).T
    b2 = np.concatenate([row(L0_ffn_sb2), np.asarray(L0_ffn_eb2).reshape(2, P)]).T
    b3 = np.concatenate([np.asarray(L0_ffn_eb3), row(L0_ffn_sb3)])
    laid = [x, *chunks(src), *chunks(dst), *chunks(edge_weight), np.asarray(L0_gnn_W).T, row(L0_gnn_b),
            L0_ffn_sW1, ew1, b1, L0_ffn_sW2, L0_ffn_eW2, b2, L0_ffn_sW3, ew3, b3, L0_ffn_gW,
            row(L0_ffn_gb)]
    names = ["x", "src", "src_tail", "dst", "dst_tail", "wgt", "wgt_tail", "gnn_wt", "gnn_b", "sw1",
             "ew1", "b1", "sw2", "ew2", "b2", "sw3", "ew3", "b3", "gate_w", "gate_b"]
    nc = bacc.Bacc("TRN2", target_bir_lowering=False, num_devices=1)
    arrays, args = {}, []
    for name, a in zip(names, laid):
        a = np.ascontiguousarray(a)
        arrays[f"in_{name}"] = a
        args.append(nc.dram_tensor(f"in_{name}", a.shape, mybir.dt.from_np(a.dtype),
                                   kind="ExternalInput").ap())
    out = nc.dram_tensor("out", (N_NODES, D), F32, kind="ExternalOutput").ap()
    build(nc, *args, out)
    return run_bass_kernel_spmd(nc, [arrays], core_ids=[0]).results[0]["out"]
```
